# Optimizing a Trainium2 kernel written in Bass

```python
import numpy as np
import jax
import jax.numpy as jnp

def _softmax(x, axis=-1):
    return jax.nn.softmax(x, axis=axis)
def _gelu(x):
    return jax.nn.gelu(x, approximate=True)
def _silu(x):
    return jax.nn.silu(x)
def _sigmoid(x):
    return jax.nn.sigmoid(x)
def _layernorm(x, axis=-1, eps=1e-5):
    m = jnp.mean(x, axis=axis, keepdims=True)
    v = jnp.var(x, axis=axis, keepdims=True)
    return (x - m) / jnp.sqrt(v + eps)
def _scatter_add(tgt, idx, src, axis=0):
    return tgt.at[idx].add(src)
def _segment_sum(src, seg, n):
    return jax.ops.segment_sum(src, seg, n)

kernel_name = 'mk_conv_preact_d1_conv_nhwc64_5b561b'

def setup_inputs(seed: int = 0):
    np.random.seed(seed)
    _w = jnp.asarray
    def _rec_inputs():
        import jax
        import jax.numpy as jnp
        _gk = jax.random.key(seed)
        x = -8.268e-05 + 0.9999 * jax.random.normal(jax.random.fold_in(_gk, 1), (16, 224, 224, 64), jnp.float32)
        return x
    x = _rec_inputs()
    def _L0_conv_setup():
        import jax, jax.numpy as jnp
        import numpy as np
        K = 1254
        key = jax.random.key(seed)
        k1, k2 = jax.random.split(key)
        x = jax.random.normal(k1, (16, 224, 224, 64), dtype=jnp.float32)
        gating_kernel = jax.random.normal(k2, (2, 2, 64, 1), dtype=jnp.float32) * 0.05
        return {'x': x, 'gating_kernel': gating_kernel}
    _L0_conv_all = _L0_conv_setup()
    _L0_conv_in = {k: v for k, v in _L0_conv_all.items() if k in ('gating_kernel', )}
    del _L0_conv_all

    return {
        "x": x,
        "L0_conv_gating_kernel": _L0_conv_in["gating_kernel"],
    }

def reference(x, L0_conv_gating_kernel):
    import jax
    import jax.numpy as jnp
    def _L0_conv_ref(x, gating_kernel):
        import jax, jax.numpy as jnp
        import numpy as np
        K = 1254
        B, H, W, C = x.shape
        kh, kw = (gating_kernel.shape[0], gating_kernel.shape[1])
        g = jax.lax.conv_general_dilated(x, gating_kernel, window_strides=(kh, kw), padding='VALID', dimension_numbers=('NHWC', 'HWIO', 'NHWC'))[..., 0]
        Ho, Wo = (g.shape[1], g.shape[2])
        n = Ho * Wo
        flat = g.reshape(B, n)
        values, indices = jax.lax.top_k(flat, K)
        batch_idx = jnp.arange(B)[:, None]
        gate = jnp.zeros((B, n), dtype=x.dtype).at[batch_idx, indices].add(values)
        gate = gate.reshape(B, Ho, Wo)
        gate_full = jnp.broadcast_to(gate[:, :, None, :, None], (B, Ho, kh, Wo, kw)).reshape(B, H, W)
        return x * gate_full[..., None]

    def _gn(v, G=32, eps=1e-5):
        B_, H_, W_, C_ = v.shape
        g = v.reshape(B_, H_, W_, G, C_ // G)
        m = jnp.mean(g, axis=(1, 2, 4), keepdims=True)
        s = jnp.var(g, axis=(1, 2, 4), keepdims=True)
        return ((g - m) / jnp.sqrt(s + eps)).reshape(v.shape)

    def _ln_c(v, eps=1e-6):
        m = jnp.mean(v, axis=-1, keepdims=True)
        s = jnp.var(v, axis=-1, keepdims=True)
        return (v - m) / jnp.sqrt(s + eps)

    def _ln_t(v, eps=1e-5):
        m = jnp.mean(v, axis=-1, keepdims=True)
        s = jnp.var(v, axis=-1, keepdims=True)
        return (v - m) / jnp.sqrt(s + eps)

    def _to_tokens(v):
        B_, H_, W_, C_ = v.shape
        return v.reshape(B_, H_ * W_, C_)
    def _from_tokens(t, like):
        return t.reshape(like.shape)

    x = x + _L0_conv_ref(_gn(x), L0_conv_gating_kernel)
    return x


_drawn_inputs = setup_inputs


def setup_inputs(seed=0):
    import zlib

    import numpy as np

    out = dict(_drawn_inputs(seed))
    spreads = {}
    factors = {}
    for name, (base, spread) in spreads.items():
        noise = np.random.default_rng([zlib.crc32(name.encode()), seed]).standard_normal(out[name].shape)
        drawn = base * np.exp(spread * noise) if base else spread * noise
        out[name] = jnp.asarray(drawn.astype(out[name].dtype))
    for name, factor in factors.items():
        out[name] = (out[name] * factor).astype(out[name].dtype)
    return out
```

```python
from contextlib import ExitStack

import numpy as np

import concourse.bass as bass
import concourse.mybir as mybir

F32 = mybir.dt.float32
BF16 = mybir.dt.bfloat16
I32 = mybir.dt.int32
ALU = mybir.AluOpType
ACT = mybir.ActivationFunctionType
AX = mybir.AxisListType

TOP = 1254
GROUPS = 32
EPS = 1e-5
BITS = 32


class Image:

    def __init__(self, half, odd, first=False):
        self.half, self.odd, self.first = half, odd, first

    def count(self, each, plus):
        return self.half * (2 * each) + (each * self.odd + plus)

    def uses(self, each):
        return self.half * each + each

    @property
    def number(self):
        return self.half * 2 + self.odd

    def next(self):
        return Image(self.half + 1, 0) if self.odd else Image(self.half, 1)


def gating_kernel(nc, x, weights, out):
    IMAGES, HEIGHT, WIDTH, CH = x.shape
    P = 128
    PA, PB = 16, 8
    ROWS = HEIGHT // PA
    CHUNKS = ROWS // 2
    BLOCKS = WIDTH // PB // 2
    STRIP = 2 * CH
    ROW = BLOCKS * STRIP
    GATES = CHUNKS * BLOCKS
    HALF = BLOCKS // 2
    TURN = HALF * P
    TURNS = 4
    IMG_TURNS = CHUNKS * TURNS
    PART = BLOCKS * GROUPS
    NORM = HEIGHT * WIDTH * (CH // GROUPS)
    SHARED = 1
    PRIVATE = ROWS - SHARED
    PAD = 32
    assert P == PA * PB and IMAGES % 2 == 0 and PART <= 512

    VECTOR_FIRST = [6, 5, 1]
    VECTOR_LATE = 3
    POOL_CHUNKS = [0, 2, 4]

    ctx = ExitStack()
    with ctx:
        def sb(name, shape, dt=F32):
            return ctx.enter_context(nc.sbuf_tensor(name, shape, dt))

        def psum(name, shape):
            return ctx.enter_context(nc.psum_tensor(name, shape, F32))

        def sem(name):
            return ctx.enter_context(nc.semaphore(name))

        xbuf = sb("xbuf", [P, 2 * PRIVATE + SHARED, ROW])
        parts = sb("parts", [P, GATES, GROUPS])
        turned = sb("turned", [P, 2, TURN])
        pool_tables = sb("pool_tables", [P, 2, PART])
        spread = sb("spread", [P, 2, BLOCKS, GROUPS])
        identity = sb("identity", [P, P])
        ones = sb("ones", [P, P])
        ones_bf = sb("ones_bf", [P, P], BF16)
        row_before = sb("row_before", [P, PA, PB], BF16)
        band_same = sb("band_same", [P, PA, PB], BF16)
        band_before = sb("band_before", [P, PA, PB], BF16)
        in_group = sb("in_group", [P, GROUPS])
        group_w = sb("group_w", [P, 2, GROUPS])
        diagonal = sb("diagonal", [P, BLOCKS + 1])
        w_col = sb("w_col", [P, 2])
        w_group = sb("w_group", [P, GROUPS])
        gate_pad = sb("gate_pad", [P, 8, PAD])
        gate_t = sb("gate_t", [P, 2 * P])
        sums = sb("sums", [P, 2, IMG_TURNS])
        sums2 = sb("sums2", [P, 2])
        group_sums = sb("group_sums", [P, 2, GROUPS])
        stat = sb("stat", [P, 5, GROUPS])
        deviation = sb("deviation", [P, GROUPS])
        shift = sb("shift", [P, 1])
        gates = sb("gates", [P, GATES])
        picked = sb("picked", [P, GATES], BF16)
        equal = sb("equal", [P, GATES], BF16)
        scanned = sb("scanned", [P, GATES], BF16)
        zeros = sb("zeros", [P, GATES], BF16)
        candidate = sb("candidate", [P, 1], I32)
        flip = sb("flip", [P, 1], I32)
        count = sb("count", [P, 1], BF16)
        eq_rows = sb("eq_rows", [P, CHUNKS], BF16)
        eq_cum = sb("eq_cum", [P, CHUNKS], BF16)
        eq_before = sb("eq_before", [P, CHUNKS], BF16)
        room = sb("room", [P, 1])
        limit = sb("limit", [P, CHUNKS])

        turn_ps = [psum(f"turn_ps{i}", [P, 1024]) for i in range(2)]
        scale_ps = psum("scale_ps", [P, 512])
        offset_ps = psum("offset_ps", [P, 512])
        parts_ps = psum("parts_ps", [P, 512])
        misc_ps = psum("misc_ps", [P, 512])
        sums_ps = misc_ps[:, 0:2 * GROUPS].rearrange("p (s g) -> p s g", s=2)
        norm_ps = misc_ps[:, 64:64 + 2 * GROUPS].rearrange("p (s g) -> p s g", s=2)
        total_ps = misc_ps[:, 128:129]
        above_ps = misc_ps[:, 129:130]
        before_ps = misc_ps[:, 136:136 + CHUNKS]
        gate_ps = misc_ps[:, 256:512]

        w_loaded = sem("w_loaded")
        settled = sem("settled")
        loaded = [[sem(f"loaded{o}_{c}") for c in range(CHUNKS)] for o in range(2)]
        stored = [[sem(f"stored{o}_{c}") for c in range(CHUNKS)] for o in range(2)]
        const_step = sem("const_step")
        w_ready = sem("w_ready")
        w_summed = sem("w_summed")
        turn_ready = sem("turn_ready")
        turn_copied = sem("turn_copied")
        turn_done = sem("turn_done")
        part_done = sem("part_done")
        parts_copied = sem("parts_copied")
        sums_ready = sem("sums_ready")
        sums_added = sem("sums_added")
        var_ready = sem("var_ready")
        dev_ready = sem("dev_ready")
        step = sem("step")
        combined = sem("combined")
        count_ready = sem("count_ready")
        total_ready = sem("total_ready")
        ties_ready = sem("ties_ready")
        ties_added = sem("ties_added")
        gate_ready = sem("gate_ready")
        gate_turned = sem("gate_turned")
        gate_copied = sem("gate_copied")
        scale_ready = sem("scale_ready")
        offset_ready = sem("offset_ready")
        vec_scaled = sem("vec_scaled")
        vec_applied = sem("vec_applied")
        tables_copied = sem("tables_copied")
        pool_scaled = sem("pool_scaled")
        pool_applied = sem("pool_applied")

        TABLE_ORDER = [POOL_CHUNKS[0]] + VECTOR_FIRST[:2] + [POOL_CHUNKS[1], VECTOR_FIRST[2],
                                                             VECTOR_LATE, POOL_CHUNKS[2]]
        VECTOR_ORDER = VECTOR_FIRST + [VECTOR_LATE]
        NV, NP = len(VECTOR_ORDER), len(POOL_CHUNKS)

        def slot(odd, row):
            return ROWS + row if odd and row < PRIVATE else row

        def x_row(odd, row):
            return xbuf[:, slot(odd, row), :]

        def rows_of(chunk):
            return [2 * chunk, 2 * chunk + 1]

        DMA_COUNT = 2 * 16

        def dram_row(t, image, row):
            v = t[image.number].rearrange("(a t) (b w) c -> a b t (w c)", a=PA, b=PB)
            return v[:, :, row, :]

        def load(eng, image, chunk, row):
            s = slot(image.odd, row)
            eng.dma_start(xbuf[:, s, :], dram_row(x, image, row))\
               .then_inc(loaded[image.odd][chunk], 16)

        def store(eng, image, chunk, row):
            s = slot(image.odd, row)
            eng.dma_start(dram_row(out, image, row), xbuf[:, s, :])\
               .then_inc(stored[image.odd][chunk], 16)

        def run(phase, turns, eng):
            last = IMAGES // 2 - 1
            first = Image(0, 0, True)
            if turns:
                turns(first)
            phase(first, None, Image(0, 1))
            with eng.Fori(0, last) as t:
                phase(Image(t, 1), Image(t, 0), Image(t + 1, 0))
                phase(Image(t + 1, 0), Image(t, 1), Image(t + 1, 1))
            phase(Image(last, 1), Image(last, 0), None)

        block = ctx.enter_context(nc.Block())

        @block.sync
        def _(sp):
            with nc.allow_non_contiguous_dma("256 weights, once"):
                sp.dma_start(w_col[:, :], weights.rearrange("kh kw c o -> (kw c) (kh o)"))\
                  .then_inc(w_loaded, 16)

            def load_chunk(image, chunk, part=None):
                for n, row in enumerate(rows_of(chunk)):
                    if part is None or n == part:
                        load(sp, image, chunk, row)

            def settle():
                sp.sem_inc(settled, 1)

            def store_chunk(image, chunk):
                if chunk in POOL_CHUNKS:
                    sp.wait_ge(pool_applied, image.count(4 * NP, 4 * POOL_CHUNKS.index(chunk) + 4))
                else:
                    sp.wait_ge(vec_applied, image.count(4 * NV, 4 * VECTOR_ORDER.index(chunk) + 4))
                settle()
                for row in rows_of(chunk):
                    store(sp, image, chunk, row)

            def freed(image, chunk):
                sp.wait_ge(stored[image.odd][chunk], image.uses(DMA_COUNT))
                settle()

            def phase(image, load1, load2):
                image1 = image.next()
                image2 = image1.next()
                store_chunk(image, 6)
                store_chunk(image, 5)
                if load1:
                    freed(image, 6)
                    load_chunk(image1, 6, 1)
                for c in [0, 1, 2, 3, 4]:
                    store_chunk(image, c)
                    if load2:
                        freed(image, c)
                        load_chunk(image2, c)
                if load2:
                    freed(image, 5)
                    load_chunk(image2, 5)
                    load_chunk(image2, 6, 0)

            first, second = Image(0, 0, True), Image(0, 1)
            for c in range(CHUNKS):
                load_chunk(first, c)
            for c in range(6):
                load_chunk(second, c)
            load_chunk(second, 6, 0)
            phase(first, True, True)
            last = IMAGES // 2 - 1
            with sp.Fori(0, last - 1) as t:
                phase(Image(t, 1), True, True)
                phase(Image(t + 1, 0), True, True)
            phase(Image(last - 1, 1), True, True)
            phase(Image(last, 0), True, False)
            phase(Image(last, 1), False, False)
            for odd in range(2):
                for c in range(CHUNKS):
                    freed(Image(last, odd), c)

        @block.gpsimd
        def _(pool):
            n = 0

            def done(ins):
                nonlocal n
                n += 1
                ins.then_inc(const_step, 1)
                pool.wait_ge(const_step, n)

            for t, v in ((identity, 0.0), (ones, 1.0), (ones_bf, 1.0), (row_before, 1.0), (band_same, 1.0),
                         (band_before, 1.0), (in_group, 1.0), (diagonal, 0.0), (gate_pad, 0.0), (zeros, 0.0)):
                done(nc.gpsimd.memset(t[:], v))

            def keep(t, base, step_q, pattern):
                done(nc.gpsimd.affine_select(out=t, in_=t, compare_op=ALU.is_ge, fill=0.0, base=base,
                                             pattern=pattern, channel_multiplier=step_q))

            def one_at_zero(t, base, pattern):
                done(nc.gpsimd.affine_select(out=t, in_=t, compare_op=ALU.not_equal, fill=1.0, base=base,
                                             pattern=pattern, channel_multiplier=1))

            one_at_zero(identity[:, :], 0, [[-1, P]])
            for j in range(0, P, 32):
                one_at_zero(diagonal[j:j + 32, :], 0, [[-1, BLOCKS + 1]])
            for j in range(0, P, CH):
                keep(in_group[j:j + CH, :], 0, 1, [[-2, GROUPS]])
                keep(in_group[j:j + CH, :], 1, -1, [[2, GROUPS]])
            keep(band_same[:], 0, 1, [[-PB, PA], [0, PB]])
            keep(band_same[:], PB - 1, -1, [[PB, PA], [0, PB]])
            keep(row_before[:], 0, 1, [[-PB, PA], [0, PB]])
            keep(row_before[:], -1, -1, [[PB, PA], [1, PB]])
            keep(band_before[:], -1, -1, [[PB, PA], [0, PB]])
            done(nc.gpsimd.memset(gate_pad[:, :, BLOCKS:BLOCKS + 1], 1.0))

            def views(odd, chunk):
                for row in (0, 1):
                    r = x_row(odd, 2 * chunk + row).rearrange("p (n w g t) -> p w n g t", n=BLOCKS, w=2, t=2)
                    for w in (0, 1):
                        yield r[:, w]

            def table(j):
                return pool_tables[:, j, :].rearrange("p (n g) -> p n g", g=GROUPS).unsqueeze(3)\
                    .to_broadcast([P, BLOCKS, GROUPS, 2])

            def phase(image, chunks):
                for k in chunks:
                    pool.wait_ge(tables_copied, image.count(2 * NP, 2 * k + 1))
                    for v in views(image.odd, POOL_CHUNKS[k]):
                        nc.gpsimd.tensor_tensor(v, v, table(0), ALU.mult).then_inc(pool_scaled, 1)
                    pool.wait_ge(tables_copied, image.count(2 * NP, 2 * k + 2))
                    for j, v in enumerate(views(image.odd, POOL_CHUNKS[k])):
                        pool.wait_ge(pool_scaled, image.count(4 * NP, 4 * k + j + 1))
                        nc.gpsimd.tensor_tensor(v, v, table(1), ALU.add).then_inc(pool_applied, 1)

            with pool.Fori(0, IMAGES // 2) as t:
                phase(Image(t, 0), range(NP))
                phase(Image(t, 1), range(NP))

        CONSTS = 10 + 1 + 4 + 4 + 5 + 1

        @block.scalar
        def _(act):
            def turn(image, k):
                ps = turn_ps[k % 2][:, 0:TURN]
                act.wait_ge(turn_ready, image.count(IMG_TURNS, k + 1))
                if k >= 2 or not image.first:
                    act.wait_ge(part_done, image.count(IMG_TURNS, k - 1))
                nc.scalar.activation(turned[:, k % 2, :], ps, ACT.Identity,
                                     accum_out=sums[:, 0, k:k + 1]).then_inc(turn_copied, 1)
                nc.scalar.activation(ps, ps, ACT.Square,
                                     accum_out=sums[:, 1, k:k + 1]).then_inc(turn_done, 1)
                if k % TURNS == 0 and k:
                    copy_parts(image, k // TURNS - 1)

            def copy_parts(image, c):
                act.wait_ge(part_done, image.count(IMG_TURNS, TURNS * (c + 1)))
                if c == 0 and not image.first:
                    act.wait_ge(combined, image.count(1, 0))
                nc.scalar.activation(parts[:, c * BLOCKS:(c + 1) * BLOCKS, :],
                                     parts_ps[:, 0:PART].rearrange("p (n g) -> p n g", g=GROUPS),
                                     ACT.Identity).then_inc(parts_copied, 1)

            def pool_tables_copy(image, k):
                n = TABLE_ORDER.index(POOL_CHUNKS[k])
                if k or not image.first:
                    act.wait_ge(pool_applied, image.count(4 * NP, 4 * k))
                for ready, ps, j in ((scale_ready, scale_ps, 0), (offset_ready, offset_ps, 1)):
                    act.wait_ge(ready, image.count(CHUNKS, n + 1))
                    nc.scalar.activation(pool_tables[:, j, :], ps[:, 0:PART], ACT.Identity)\
                      .then_inc(tables_copied, 1)

            def phase(image, before, after):
                act.wait_ge(var_ready, image.count(1, 1))
                nc.scalar.activation(deviation[:, :], stat[:, 2, :], ACT.Sqrt).then_inc(dev_ready, 1)
                if after:
                    for k in range(8):
                        turn(after, k)
                if before:
                    pool_tables_copy(before, 2)
                if after:
                    for k in range(8, 16):
                        turn(after, k)
                pool_tables_copy(image, 0)
                if after:
                    for k in range(16, 20):
                        turn(after, k)
                pool_tables_copy(image, 1)
                if after:
                    for k in range(20, IMG_TURNS):
                        turn(after, k)
                    copy_parts(after, CHUNKS - 1)

            def all_turns(image):
                for k in range(IMG_TURNS):
                    turn(image, k)
                copy_parts(image, CHUNKS - 1)

            run(phase, all_turns, act)
            pool_tables_copy(Image(IMAGES // 2 - 1, 1), 2)

        @block.tensor
        def _(pe):
            pe.wait_ge(const_step, CONSTS)
            pe.wait_ge(w_ready, 1)
            for row in (0, 1):
                mm = nc.tensor.matmul(norm_ps[:, 0, :], ones[:, :], group_w[:, row, :], start=row == 0, stop=row == 1)
            mm.then_inc(w_summed, 1)

            def transposes(image, k):
                chunk, half, row = k // TURNS, k % TURNS // 2, k % 2
                if k % TURNS == 0:
                    pe.wait_ge(loaded[image.odd][chunk], image.uses(DMA_COUNT))
                if k >= 2 or not image.first:
                    pe.wait_ge(turn_done, image.count(IMG_TURNS, k - 1))
                r = x_row(image.odd, 2 * chunk + row)
                for j in range(HALF):
                    n = half * HALF + j
                    mm = nc.tensor.transpose(turn_ps[k % 2][:, j * P:(j + 1) * P], r[:, n * STRIP:(n + 1) * STRIP],
                                             identity[:, :])
                mm.then_inc(turn_ready, 1)

            def products(image, k):
                chunk, half, row = k // TURNS, k % TURNS // 2, k % 2
                if k % TURNS == 0 and (chunk or not image.first):
                    pe.wait_ge(parts_copied, image.count(CHUNKS, chunk))
                pe.wait_ge(turn_copied, image.count(IMG_TURNS, k + 1))
                for j in range(HALF):
                    n = half * HALF + j
                    mm = nc.tensor.matmul(parts_ps[:, n * GROUPS:(n + 1) * GROUPS], turned[:, k % 2, j * P:(j + 1) * P],
                                          group_w[:, row, :], start=(k % TURNS == 0 and j == 0),
                                          stop=(k % TURNS == TURNS - 1 and j == HALF - 1), skip_group_check=True)
                mm.then_inc(part_done, 1)

            def turn(image, k):
                transposes(image, k)
                if k:
                    products(image, k - 1)
                if k == IMG_TURNS - 1:
                    products(image, k)

            def tables(image, n):
                chunk = TABLE_ORDER[n]
                q, half = chunk % 4, chunk // 4
                for ready, ps, j in ((scale_ready, scale_ps, 0), (offset_ready, offset_ps, 1)):
                    if n or not image.first:
                        prev = TABLE_ORDER[n - 1]
                        if prev in POOL_CHUNKS:
                            pe.wait_ge(tables_copied, image.count(2 * NP, 2 * POOL_CHUNKS.index(prev) + j + 1 - (0 if n else 2 * NP)))
                        else:
                            pe.wait_ge(vec_scaled if j == 0 else vec_applied,
                                       image.count(4 * NV, 4 * VECTOR_ORDER.index(prev) + 4))
                    nc.tensor.matmul(ps[:, 0:PART], gate_t[q * 32:q * 32 + BLOCKS + 1, half * P:(half + 1) * P],
                                     spread[q * 32:q * 32 + BLOCKS + 1, j, :, :].rearrange("p n g -> p (n g)"),
                                     start=True, stop=True).then_inc(ready, 1)

            def phase(image, before, after):
                pe.wait_ge(sums_ready, image.count(1, 1))
                nc.tensor.matmul(misc_ps[:, 0:2 * GROUPS], ones[:, :], group_sums[:, :, :].rearrange("p s g -> p (s g)"),
                                 start=True, stop=True).then_inc(sums_added, 1)
                if before:
                    tables(before, 5)
                for r in range(BITS):
                    pe.wait_ge(count_ready, image.count(BITS, r + 1))
                    nc.tensor.matmul(total_ps, ones_bf[:, :], count[:, :], start=True, stop=True)\
                      .then_inc(total_ready, 1)
                    if after and r % 2 == 1 and r < 16:
                        turn(after, r // 2)
                    if before and r == 16:
                        tables(before, 6)
                    if after and r % 2 == 1 and r >= 16:
                        turn(after, r // 2)
                pe.wait_ge(ties_ready, image.count(1, 1))
                nc.tensor.matmul(above_ps, ones_bf[:, :], count[:, :], start=True, stop=True)
                flat = "q a b -> q (a b)"
                nc.tensor.matmul(before_ps, row_before[:].rearrange(flat), eq_rows[:, :], start=True, stop=False)
                nc.tensor.matmul(before_ps, band_same[:].rearrange(flat), eq_before[:, :], start=False, stop=False)
                nc.tensor.matmul(before_ps, band_before[:].rearrange(flat),
                                 eq_cum[:, CHUNKS - 1:CHUNKS].to_broadcast([P, CHUNKS]), start=False, stop=True)\
                  .then_inc(ties_added, 1)
                pe.wait_ge(gate_ready, image.count(1, 1))
                for h in (0, 1):
                    mm = nc.tensor.transpose(gate_ps[:, h * P:(h + 1) * P],
                                             gate_pad[:, 4 * h:4 * h + 4, :].rearrange("p k n -> p (k n)"), identity[:, :])
                mm.then_inc(gate_turned, 1)
                pe.wait_ge(gate_copied, image.count(1, 1))
                tables(image, 0)
                tables(image, 1)
                if after:
                    for k in range(16, 18):
                        turn(after, k)
                tables(image, 2)
                if after:
                    for k in range(18, 20):
                        turn(after, k)
                tables(image, 3)
                tables(image, 4)
                if after:
                    for k in range(20, IMG_TURNS):
                        turn(after, k)

            def all_turns(image):
                for k in range(IMG_TURNS):
                    turn(image, k)

            run(phase, all_turns, pe)
            final = Image(IMAGES // 2 - 1, 1)
            tables(final, 5)
            tables(final, 6)

        @block.vector
        def _(dve):
            dve.wait_ge(w_loaded, 16)
            dve.wait_ge(const_step, CONSTS)
            for row in (0, 1):
                ins = nc.vector.tensor_scalar(group_w[:, row, :], in_group[:, :], w_col[:, row:row + 1], None, ALU.mult)
            ins.then_inc(w_ready, 1)
            dve.wait_ge(w_summed, 1)
            nc.vector.tensor_copy(w_group[:, :], norm_ps[:, 0, :])

            def bulk(image, n):
                chunk = VECTOR_ORDER[n]
                views = []
                for row in (0, 1):
                    r = x_row(image.odd, 2 * chunk + row).rearrange("p (n w g t) -> p w n g t", n=BLOCKS, w=2, t=2)
                    views += [r[:, 0], r[:, 1]]

                def table(ps):
                    return ps[:, 0:PART].rearrange("p (n g) -> p n g", g=GROUPS).unsqueeze(3)\
                        .to_broadcast([P, BLOCKS, GROUPS, 2])

                k = TABLE_ORDER.index(chunk)
                for j, v in enumerate(views):
                    if j == 0:
                        dve.wait_ge(scale_ready, image.count(CHUNKS, k + 1))
                    nc.vector.tensor_tensor(v, v, table(scale_ps), ALU.mult).then_inc(vec_scaled, 1)
                    yield
                for j, v in enumerate(views):
                    if j == 0:
                        dve.wait_ge(offset_ready, image.count(CHUNKS, k + 1))
                    dve.wait_ge(vec_scaled, image.count(4 * NV, 4 * n + j + 1))
                    nc.vector.tensor_tensor(v, v, table(offset_ps), ALU.add).then_inc(vec_applied, 1)
                    yield

            def phase(image, before, after):
                steps = 0

                def chain(ins):
                    nonlocal steps
                    steps += 1
                    ins.then_inc(step, 1)
                    dve.wait_ge(step, image.count(STEPS, steps))

                def rows(t):
                    return t[:, :].rearrange("p (k n) -> p k n", n=BLOCKS)

                dve.wait_ge(turn_done, image.count(IMG_TURNS, IMG_TURNS))
                chain(nc.vector.tensor_reduce(sums2[:, :], sums[:, :, :], AX.X, ALU.add))
                nc.vector.tensor_tensor(group_sums[:, :, :], in_group[:, :].unsqueeze(1).to_broadcast([P, 2, GROUPS]),
                                        sums2[:, :].unsqueeze(2).to_broadcast([P, 2, GROUPS]), ALU.mult)\
                  .then_inc(sums_ready, 1)
                dve.wait_ge(sums_added, image.count(1, 1))
                chain(nc.vector.tensor_scalar(stat[:, 0:2, :], sums_ps, 1.0 / NORM, None, ALU.mult))
                chain(nc.vector.tensor_tensor(stat[:, 3, :], stat[:, 0, :], stat[:, 0, :], ALU.mult))
                chain(nc.vector.tensor_tensor(stat[:, 4, :], stat[:, 1, :], stat[:, 3, :], ALU.subtract))
                nc.vector.tensor_scalar(stat[:, 2, :], stat[:, 4, :], 0.0, EPS, ALU.max, ALU.add).then_inc(var_ready, 1)
                dve.wait_ge(dev_ready, image.count(1, 1))
                chain(nc.vector.reciprocal(stat[:, 1, :], deviation[:, :]))
                chain(nc.vector.tensor_tensor(stat[:, 3, :], stat[:, 1, :], stat[:, 1, :], ALU.mult))
                chain(nc.vector.tensor_tensor(stat[:, 4, :], stat[:, 3, :], stat[:, 2, :], ALU.mult))
                chain(nc.vector.tensor_scalar(stat[:, 4, :], stat[:, 4, :], -0.5, 1.5, ALU.mult, ALU.add))
                nc.vector.tensor_tensor(norm_ps[:, 0, :], stat[:, 1, :], stat[:, 4, :], ALU.mult)
                chain(nc.vector.tensor_tensor(stat[:, 1, :], stat[:, 1, :], stat[:, 4, :], ALU.mult))
                chain(nc.vector.scalar_tensor_tensor(stat[:, 3, :], stat[:, 0, :], -1.0, stat[:, 1, :], ALU.mult, ALU.mult))
                nc.vector.tensor_copy(norm_ps[:, 1, :], stat[:, 3, :])
                chain(nc.vector.scalar_tensor_tensor(stat[:, 4, :], stat[:, 3, :], 1.0, w_group[:, :], ALU.mult,
                                                     ALU.mult, accum_out=shift[:, :]))
                dve.wait_ge(parts_copied, image.count(CHUNKS, CHUNKS))
                chain(nc.vector.tensor_tensor(parts[:, :, :], parts[:, :, :],
                                              norm_ps[:, 0:1, :].to_broadcast([P, GATES, GROUPS]), ALU.mult))
                ins = nc.vector.tensor_reduce(gates[:, :], parts[:, :, :], AX.X, ALU.add)
                ins.then_inc(combined, 1)
                dve.wait_ge(combined, image.count(1, 1))
                chain(nc.vector.tensor_scalar(gates[:, :], gates[:, :], shift[:, 0:1], None, ALU.add))
                chain(nc.vector.memset(candidate[:, :], 0))
                work = bulk(before, NV - 1) if before else iter(())
                for r in range(BITS):
                    nc.vector.tensor_scalar(picked[:, :], gates[:, :], candidate[:, 0:1].bitcast(F32), None, ALU.is_ge,
                                            ALU.add, accum_out=count[:, :]).then_inc(count_ready, 1)
                    if r % 2 == 0 and r < 16:
                        next(work, None)
                    dve.wait_ge(total_ready, image.count(BITS, r + 1))
                    chain(nc.vector.tensor_scalar(flip[:, :], total_ps, float(TOP), float(2 ** (31 - r)) if r else -1.0,
                                                  ALU.is_lt, ALU.mult))
                    next_bit = 2 ** (30 - r) if r < BITS - 1 else 0
                    chain(nc.vector.scalar_tensor_tensor(candidate[:, :], candidate[:, :], next_bit, flip[:, :],
                                                         ALU.bitwise_xor, ALU.bitwise_xor))
                for _ in work:
                    pass
                kth = candidate[:, 0:1].bitcast(F32)
                nc.vector.tensor_scalar(picked[:, :], gates[:, :], kth, None, ALU.is_gt, ALU.add, accum_out=count[:, :])
                chain(nc.vector.tensor_scalar(equal[:, :], gates[:, :], kth, None, ALU.is_equal))
                with nc.allow_low_precision("counts up to BLOCKS are exact in bfloat16"):
                    chain(nc.vector.tensor_reduce(eq_rows[:, :], rows(equal), AX.X, ALU.add))
                chain(nc.vector.tensor_tensor_scan(eq_cum[:, :], eq_rows[:, :], zeros[:, 0:CHUNKS], 0.0, ALU.add, ALU.add))
                nc.vector.tensor_tensor(eq_before[:, :], eq_cum[:, :], eq_rows[:, :], ALU.subtract).then_inc(ties_ready, 1)
                nc.vector.tensor_tensor_scan(scanned[:, :], equal[:, :], zeros[:, :], 0.0, ALU.add, ALU.add)
                dve.wait_ge(ties_added, image.count(1, 1))
                chain(nc.vector.tensor_scalar(room[:, :], above_ps, -1.0, float(TOP), ALU.mult, ALU.add))
                chain(nc.vector.tensor_tensor(limit[:, :], before_ps, eq_before[:, :], ALU.subtract))
                chain(nc.vector.tensor_scalar(limit[:, :], limit[:, :], -1.0, room[:, 0:1], ALU.mult, ALU.add))
                chain(nc.vector.tensor_tensor(rows(scanned), rows(scanned),
                                              limit[:, :].unsqueeze(2).to_broadcast([P, CHUNKS, BLOCKS]), ALU.is_le))
                chain(nc.vector.tensor_tensor(equal[:, :], equal[:, :], scanned[:, :], ALU.mult))
                chain(nc.vector.tensor_tensor(picked[:, :], picked[:, :], equal[:, :], ALU.add))
                if before:
                    dve.wait_ge(offset_ready, image.count(CHUNKS, 0))
                d = diagonal[:, 0:BLOCKS].unsqueeze(2).to_broadcast([P, BLOCKS, GROUPS])
                for j in (0, 1):
                    ins = nc.vector.tensor_tensor(spread[:, j, :, :], d, norm_ps[:, j:j + 1, :].to_broadcast([P, BLOCKS, GROUPS]),
                                                  ALU.mult)
                chain(ins)
                chain(nc.vector.tensor_scalar(spread[:, 0, :, :], spread[:, 0, :, :], diagonal[:, BLOCKS:BLOCKS + 1], None, ALU.add))
                nc.vector.tensor_tensor(gate_pad[:, 0:CHUNKS, 0:BLOCKS], rows(gates), rows(picked), ALU.mult)\
                  .then_inc(gate_ready, 1)
                dve.wait_ge(gate_turned, image.count(1, 1))
                nc.vector.tensor_copy(gate_t[:, :], gate_ps).then_inc(gate_copied, 1)
                for n in range(NV - 1):
                    for _ in bulk(image, n):
                        pass
                assert steps == STEPS, steps

            STEPS = 25 + 2 * BITS
            run(phase, None, dve)
            for _ in bulk(Image(IMAGES // 2 - 1, 1), NV - 1):
                pass


def kernel(**inputs):
    import concourse.bacc as bacc
    from concourse.bass_utils import run_bass_kernel_spmd

    nc = bacc.Bacc("TRN2", target_bir_lowering=False, num_devices=1,
                    dynamic_dma_scratch_size=1024)
    arrays, args = {}, []
    for name in ("x", "L0_conv_gating_kernel"):
        a = np.ascontiguousarray(inputs[name])
        arrays[name] = a
        args.append(nc.dram_tensor(name, a.shape, mybir.dt.from_np(a.dtype), kind="ExternalInput").ap())
    args.append(nc.dram_tensor("out", arrays["x"].shape, F32, kind="ExternalOutput").ap())
    gating_kernel(nc, *args)
    return run_bass_kernel_spmd(nc, [arrays], core_ids=[0]).results[0]["out"]
```

```python
from contextlib import ExitStack

import numpy as np

import concourse.bass as bass
import concourse.mybir as mybir

F32 = mybir.dt.float32
BF16 = mybir.dt.bfloat16
I32 = mybir.dt.int32
ALU = mybir.AluOpType
ACT = mybir.ActivationFunctionType
AX = mybir.AxisListType

TOP = 1254
GROUPS = 32
EPS = 1e-5
BITS = 32


class Image:

    def __init__(self, half, odd, first=False):
        self.half, self.odd, self.first = half, odd, first

    def count(self, each, plus):
        return self.half * (2 * each) + (each * self.odd + plus)

    def uses(self, each):
        return self.half * each + each

    @property
    def number(self):
        return self.half * 2 + self.odd

    def next(self):
        return Image(self.half + 1, 0) if self.odd else Image(self.half, 1)


def gating_kernel(nc, x, weights, out):
    IMAGES, HEIGHT, WIDTH, CH = x.shape
    P = 128
    PA, PB = 16, 8
    ROWS = HEIGHT // PA
    CHUNKS = ROWS // 2
    BLOCKS = WIDTH // PB // 2
    STRIP = 2 * CH
    ROW = BLOCKS * STRIP
    GATES = CHUNKS * BLOCKS
    SQ = 32
    QUADS = P // SQ
    TURN = ROW // 2
    TURNS = 4
    IMG_TURNS = CHUNKS * TURNS
    PART = BLOCKS * GROUPS
    NORM = HEIGHT * WIDTH * (CH // GROUPS)
    SHARED = 2
    PRIVATE = ROWS - SHARED
    PAD = 32
    assert P == PA * PB and IMAGES % 2 == 0 and PART <= 512

    VECTOR_ORDER = [6, 0, 4]
    VECTOR_LATE = VECTOR_ORDER[-1]
    POOL_CHUNKS = [1, 2, 3, 5]
    TABLE_ORDER = [1, 6, 0, 2, 3, 4, 5]
    STORE_ORDER = [1, 0, 2, 3, 4, 5]
    AT_ONCE = 4
    LATE_TURNS = 4

    ctx = ExitStack()
    with ctx:
        def sb(name, shape, dt=F32):
            return ctx.enter_context(nc.sbuf_tensor(name, shape, dt))

        def psum(name, shape):
            return ctx.enter_context(nc.psum_tensor(name, shape, F32))

        def sem(name):
            return ctx.enter_context(nc.semaphore(name))

        xbuf = sb("xbuf", [P, 2 * PRIVATE + SHARED, ROW])
        parts = sb("parts", [P, GATES, GROUPS])
        turned = sb("turned", [P, 2, TURN])
        unused = sb("unused", [P, TURN], BF16)
        pool_tables = sb("pool_tables", [P, 2, PART])
        spread = sb("spread", [P, 2, BLOCKS, GROUPS])
        identity = sb("identity", [P, P])
        ones = sb("ones", [P, P])
        ones_bf = sb("ones_bf", [P, P], BF16)
        row_before = sb("row_before", [P, PA, PB], BF16)
        band_same = sb("band_same", [P, PA, PB], BF16)
        band_before = sb("band_before", [P, PA, PB], BF16)
        quad_same = sb("quad_same", [P, QUADS, SQ], BF16)
        combine_w = sb("combine_w", [P, QUADS, SQ])
        in_group = sb("in_group", [P, GROUPS // 2])
        group_w = sb("group_w", [P, 2, 2, 2, QUADS, GROUPS])
        diagonal = sb("diagonal", [P, SQ])
        w_col = sb("w_col", [P, 2, 2, 2])
        w_group = sb("w_group", [P, GROUPS])
        gate_pad = sb("gate_pad", [P, 8, PAD])
        gate_t = sb("gate_t", [P, 2 * P])
        sums = sb("sums", [P, 2, 2, ROWS])
        sums2 = sb("sums2", [P, 2, 2])
        own = sb("own", [P, 1])
        group_sums = sb("group_sums", [P, 2, GROUPS])
        stat = sb("stat", [P, 5, GROUPS])
        deviation = sb("deviation", [P, GROUPS])
        shift = sb("shift", [P, 1])
        gates = sb("gates", [P, GATES])
        picked = sb("picked", [P, GATES], BF16)
        equal = sb("equal", [P, GATES], BF16)
        scanned = sb("scanned", [P, GATES], BF16)
        zeros = sb("zeros", [P, GATES], BF16)
        candidate = sb("candidate", [P, 1], I32)
        flip = sb("flip", [P, 1], I32)
        count = sb("count", [P, 1], BF16)
        eq_rows = sb("eq_rows", [P, CHUNKS], BF16)
        eq_cum = sb("eq_cum", [P, CHUNKS], BF16)
        eq_before = sb("eq_before", [P, CHUNKS], BF16)
        room = sb("room", [P, 1])
        limit = sb("limit", [P, CHUNKS])

        combine_ps = [psum(f"combine_ps{i}", [P, 512]) for i in range(2)]
        scale_ps = psum("scale_ps", [P, 512])
        offset_ps = psum("offset_ps", [P, 512])
        parts_ps = [psum(f"parts_ps{i}", [P, 512]) for i in range(2)]
        misc_ps = psum("misc_ps", [P, 512])
        sums_ps = misc_ps[:, 0:2 * GROUPS].rearrange("p (s g) -> p s g", s=2)
        norm_ps = misc_ps[:, 64:64 + 2 * GROUPS].rearrange("p (s g) -> p s g", s=2)
        total_ps = misc_ps[:, 128:129]
        above_ps = misc_ps[:, 129:130]
        before_ps = misc_ps[:, 136:136 + CHUNKS]
        gate_ps = misc_ps[:, 256:512]

        w_loaded = sem("w_loaded")
        settled = sem("settled")
        loaded = [[sem(f"loaded{o}_{c}") for c in range(CHUNKS)] for o in range(2)]
        stored = [[sem(f"stored{o}_{c}") for c in range(CHUNKS)] for o in range(2)]
        const_step = sem("const_step")
        w_ready = sem("w_ready")
        w_summed = sem("w_summed")
        turn_ready = sem("turn_ready")
        turn_done = sem("turn_done")
        turn_summed = sem("turn_summed")
        part_done = sem("part_done")
        combine_ready = sem("combine_ready")
        combine_done = sem("combine_done")
        combine_read = sem("combine_read")
        parts_copied = sem("parts_copied")
        sums_ready = sem("sums_ready")
        sums_added = sem("sums_added")
        var_ready = sem("var_ready")
        dev_ready = sem("dev_ready")
        step = sem("step")
        combined = sem("combined")
        count_ready = sem("count_ready")
        total_ready = sem("total_ready")
        ties_ready = sem("ties_ready")
        ties_added = sem("ties_added")
        gate_ready = sem("gate_ready")
        gate_turned = sem("gate_turned")
        gate_copied = sem("gate_copied")
        scale_ready = sem("scale_ready")
        offset_ready = sem("offset_ready")
        vec_scaled = sem("vec_scaled")
        vec_applied = sem("vec_applied")
        tables_copied = sem("tables_copied")
        pool_scaled = sem("pool_scaled")
        pool_applied = sem("pool_applied")

        NV, NP = len(VECTOR_ORDER), len(POOL_CHUNKS)

        def slot(odd, row):
            return ROWS + row if odd and row < PRIVATE else row

        def x_row(odd, row):
            return xbuf[:, slot(odd, row), :]

        def rows_of(chunk):
            return [2 * chunk, 2 * chunk + 1]

        DMA_COUNT = 2 * 16

        def dram_row(t, image, row):
            v = t[image.number].rearrange("(a t) (b w) c -> a b t (w c)", a=PA, b=PB)
            return v[:, :, row, :]

        def load(eng, image, chunk, row):
            s = slot(image.odd, row)
            eng.dma_start(xbuf[:, s, :], dram_row(x, image, row))\
               .then_inc(loaded[image.odd][chunk], 16)

        def store(eng, image, chunk, row):
            s = slot(image.odd, row)
            eng.dma_start(dram_row(out, image, row), xbuf[:, s, :])\
               .then_inc(stored[image.odd][chunk], 16)

        def run(phase, turns, eng):
            last = IMAGES // 2 - 1
            first = Image(0, 0, True)
            if turns:
                for k in range(IMG_TURNS):
                    turns(first, k)
            phase(first, None, Image(0, 1))
            with eng.Fori(0, last) as t:
                phase(Image(t, 1), Image(t, 0), Image(t + 1, 0))
                phase(Image(t + 1, 0), Image(t, 1), Image(t + 1, 1))
            phase(Image(last, 1), Image(last, 0), None)

        block = ctx.enter_context(nc.Block())

        @block.sync
        def _(sp):
            with nc.allow_non_contiguous_dma("256 weights, once"):
                for i in range(QUADS):
                    for kh in range(2):
                        sp.dma_start(w_col[i * SQ:(i + 1) * SQ, kh], weights[kh].rearrange(
                            "kw (h u) o -> u kw (h o)", u=SQ)).then_inc(w_loaded, 16)

            def load_chunk(image, chunk, part=None):
                for n, row in enumerate(rows_of(chunk)):
                    if part is None or n == part:
                        load(sp, image, chunk, row)

            def settle():
                sp.sem_inc(settled, 1)

            def store_chunk(image, chunk):
                if chunk in POOL_CHUNKS:
                    sp.wait_ge(pool_applied, image.count(4 * NP, 4 * POOL_CHUNKS.index(chunk) + 4))
                else:
                    sp.wait_ge(vec_applied, image.count(4 * NV, 4 * VECTOR_ORDER.index(chunk) + 4))
                settle()
                for row in rows_of(chunk):
                    store(sp, image, chunk, row)

            def freed(image, chunk):
                sp.wait_ge(stored[image.odd][chunk], image.uses(DMA_COUNT))
                settle()

            def phase(image, load1, load2):
                image1 = image.next()
                image2 = image1.next()
                store_chunk(image, 6)
                if load1:
                    freed(image, 6)
                    load_chunk(image1, 6)
                for c in STORE_ORDER:
                    store_chunk(image, c)
                    if load2:
                        freed(image, c)
                        load_chunk(image2, c)

            first, second = Image(0, 0, True), Image(0, 1)
            for c in range(CHUNKS):
                load_chunk(first, c)
            for c in range(6):
                load_chunk(second, c)
            phase(first, True, True)
            last = IMAGES // 2 - 1
            with sp.Fori(0, last - 1) as t:
                phase(Image(t, 1), True, True)
                phase(Image(t + 1, 0), True, True)
            phase(Image(last - 1, 1), True, True)
            phase(Image(last, 0), True, False)
            phase(Image(last, 1), False, False)
            for odd in range(2):
                for c in range(CHUNKS):
                    freed(Image(last, odd), c)

        CONSTS = 12 + 1 + 4 * 3 + 2 + 8 * 4 + 5 + 1

        @block.gpsimd
        def _(pool):
            n = 0

            def done(ins):
                nonlocal n
                n += 1
                ins.then_inc(const_step, 1)
                pool.wait_ge(const_step, n)

            for t, v in ((identity, 0.0), (ones, 1.0), (ones_bf, 1.0), (row_before, 1.0), (band_same, 1.0),
                         (band_before, 1.0), (in_group, 1.0), (diagonal, 0.0), (gate_pad, 0.0), (zeros, 0.0),
                         (quad_same, 1.0), (group_w, 1.0)):
                done(nc.gpsimd.memset(t[:], v))

            def keep(t, base, step_q, pattern):
                done(nc.gpsimd.affine_select(out=t, in_=t, compare_op=ALU.is_ge, fill=0.0, base=base,
                                             pattern=pattern, channel_multiplier=step_q))

            def one_at_zero(t, base, pattern):
                done(nc.gpsimd.affine_select(out=t, in_=t, compare_op=ALU.not_equal, fill=1.0, base=base,
                                             pattern=pattern, channel_multiplier=1))

            one_at_zero(identity[:, :], 0, [[-1, P]])
            for j in range(0, P, 32):
                one_at_zero(diagonal[j:j + 32, :], 0, [[-1, SQ]])
                keep(in_group[j:j + 32, :], 0, 1, [[-2, GROUPS // 2]])
                keep(in_group[j:j + 32, :], 1, -1, [[2, GROUPS // 2]])
            keep(quad_same[:], 0, 1, [[-SQ, QUADS], [0, SQ]])
            keep(quad_same[:], SQ - 1, -1, [[SQ, QUADS], [0, SQ]])
            for kh in (0, 1):
                for kw in (0, 1):
                    for h in (0, 1):
                        w = group_w[:, kh, kw, h]
                        keep(w, 0, 1, [[-SQ, QUADS], [0, GROUPS]])
                        keep(w, SQ - 1, -1, [[SQ, QUADS], [0, GROUPS]])
                        keep(w, SQ * h, 1, [[-SQ, QUADS], [-2, GROUPS]])
                        keep(w, 1 - SQ * h, -1, [[SQ, QUADS], [2, GROUPS]])
            keep(band_same[:], 0, 1, [[-PB, PA], [0, PB]])
            keep(band_same[:], PB - 1, -1, [[PB, PA], [0, PB]])
            keep(row_before[:], 0, 1, [[-PB, PA], [0, PB]])
            keep(row_before[:], -1, -1, [[PB, PA], [1, PB]])
            keep(band_before[:], -1, -1, [[PB, PA], [0, PB]])
            done(nc.gpsimd.memset(gate_pad[:, :, BLOCKS:BLOCKS + 1], 1.0))

            def views(odd, chunk):
                for row in (0, 1):
                    r = x_row(odd, 2 * chunk + row).rearrange("p (n w g t) -> p w n g t", n=BLOCKS, w=2, t=2)
                    for w in (0, 1):
                        yield r[:, w]

            def table(j):
                return pool_tables[:, j, :].rearrange("p (n g) -> p n g", g=GROUPS).unsqueeze(3)\
                    .to_broadcast([P, BLOCKS, GROUPS, 2])

            def phase(image, chunks):
                for k in chunks:
                    pool.wait_ge(tables_copied, image.count(2 * NP, 2 * k + 1))
                    for v in views(image.odd, POOL_CHUNKS[k]):
                        nc.gpsimd.tensor_tensor(v, v, table(0), ALU.mult).then_inc(pool_scaled, 1)
                    pool.wait_ge(tables_copied, image.count(2 * NP, 2 * k + 2))
                    for j, v in enumerate(views(image.odd, POOL_CHUNKS[k])):
                        pool.wait_ge(pool_scaled, image.count(4 * NP, 4 * k + j + 1))
                        nc.gpsimd.tensor_tensor(v, v, table(1), ALU.add).then_inc(pool_applied, 1)

            assert n == CONSTS, n
            with pool.Fori(0, IMAGES // 2) as t:
                phase(Image(t, 0), range(NP))
                phase(Image(t, 1), range(NP))

        @block.scalar
        def _(act):
            def turn(image, k):
                y, row, h = turned[:, k % 2, :], k // 2, k % 2
                act.wait_ge(turn_ready, image.count(IMG_TURNS, k + 1))
                if k or not image.first:
                    act.wait_ge(turn_done, image.count(IMG_TURNS, k))
                nc.scalar.activation(unused[:, :], y, ACT.Identity,
                                     accum_out=sums[:, 0, h, row:row + 1]).then_inc(turn_summed, 1)
                act.wait_ge(turn_summed, image.count(IMG_TURNS, k + 1))
                nc.scalar.activation(unused[:, :], y, ACT.Square,
                                     accum_out=sums[:, 1, h, row:row + 1]).then_inc(turn_done, 1)
                if k % TURNS == 1 and k > 1:
                    copy_parts(image, k // TURNS - 1)
                if k == IMG_TURNS - 1:
                    copy_parts(image, CHUNKS - 1)

            def copy_parts(image, c):
                act.wait_ge(part_done, image.count(IMG_TURNS, TURNS * (c + 1)))
                if c == 0 and not image.first:
                    act.wait_ge(combined, image.count(1, 0))
                nc.scalar.activation(parts[:, c * BLOCKS:(c + 1) * BLOCKS, :],
                                     parts_ps[(c + image.odd * CHUNKS) % 2][:, 0:PART]
                                     .rearrange("p (n g) -> p n g", g=GROUPS),
                                     ACT.Identity).then_inc(parts_copied, 1)

            def pool_tables_copy(image, k):
                n = TABLE_ORDER.index(POOL_CHUNKS[k])
                if k or not image.first:
                    act.wait_ge(pool_applied, image.count(4 * NP, 4 * k))
                for ready, ps, j in ((scale_ready, scale_ps, 0), (offset_ready, offset_ps, 1)):
                    act.wait_ge(ready, image.count(CHUNKS, n + 1))
                    nc.scalar.activation(pool_tables[:, j, :], ps[:, 0:PART], ACT.Identity)\
                      .then_inc(tables_copied, 1)

            def phase(image, before, after):
                act.wait_ge(var_ready, image.count(1, 1))
                nc.scalar.activation(deviation[:, :], stat[:, 2, :], ACT.Sqrt).then_inc(dev_ready, 1)
                if before:
                    pool_tables_copy(before, 2)
                if after:
                    for k in range(8):
                        turn(after, k)
                if before:
                    pool_tables_copy(before, 3)
                if after:
                    for k in range(8, IMG_TURNS - LATE_TURNS):
                        turn(after, k)
                pool_tables_copy(image, 0)
                pool_tables_copy(image, 1)
                if after:
                    for k in range(IMG_TURNS - LATE_TURNS, IMG_TURNS):
                        turn(after, k)

            run(phase, turn, act)
            final = Image(IMAGES // 2 - 1, 1)
            pool_tables_copy(final, 2)
            pool_tables_copy(final, 3)

        @block.tensor
        def _(pe):
            pe.wait_ge(const_step, CONSTS)
            pe.wait_ge(w_ready, 1)
            for n in range(8):
                w = group_w[:, n // 4, n // 2 % 2, n % 2].rearrange("p i g -> p (i g)")
                mm = nc.tensor.matmul(misc_ps[:, 0:P], ones[:, :], w, start=n == 0, stop=n == 7)
            mm.then_inc(w_summed, 1)

            def turn(image, k):
                chunk, row, h = k // TURNS, k // 2 % 2, k % 2
                if k % TURNS == 0 and (chunk >= 2 or not image.first):
                    pe.wait_ge(parts_copied, image.count(CHUNKS, chunk - 1))
                pe.wait_ge(turn_ready, image.count(IMG_TURNS, k + 1))
                y = turned[:, k % 2, :].rearrange("p (n w v) -> p w n v", w=2, v=SQ)
                for kw in (0, 1):
                    mm = nc.tensor.matmul(parts_ps[(chunk + image.odd * CHUNKS) % 2][:, 0:PART],
                                          group_w[:, row, kw, h].rearrange("p i g -> p (i g)"), y[:, kw],
                                          start=(k % TURNS == 0 and kw == 0), stop=(k % TURNS == TURNS - 1 and kw == 1))
                mm.then_inc(part_done, 1)

            def tables(image, n):
                chunk = TABLE_ORDER[n]
                q, half = chunk % 4, chunk // 4
                for ready, ps, j in ((scale_ready, scale_ps, 0), (offset_ready, offset_ps, 1)):
                    if n or not image.first:
                        prev = TABLE_ORDER[n - 1]
                        if prev in POOL_CHUNKS:
                            pe.wait_ge(tables_copied, image.count(2 * NP, 2 * POOL_CHUNKS.index(prev) + j + 1 - (0 if n else 2 * NP)))
                        else:
                            pe.wait_ge(vec_scaled if j == 0 else vec_applied,
                                       image.count(4 * NV, 4 * VECTOR_ORDER.index(prev) + 4))
                    nc.tensor.matmul(ps[:, 0:PART], gate_t[q * 32:q * 32 + BLOCKS + 1, half * P:(half + 1) * P],
                                     spread[q * 32:q * 32 + BLOCKS + 1, j, :, :].rearrange("p n g -> p (n g)"),
                                     start=True, stop=True).then_inc(ready, 1)

            def phase(image, before, after):
                pe.wait_ge(sums_ready, image.count(1, 1))
                nc.tensor.matmul(misc_ps[:, 0:2 * GROUPS], ones[:, :], group_sums[:, :, :].rearrange("p s g -> p (s g)"),
                                 start=True, stop=True).then_inc(sums_added, 1)
                pe.wait_ge(combine_ready, image.count(1, 1))
                pe.wait_ge(parts_copied, image.count(CHUNKS, CHUNKS))
                for c in range(CHUNKS):
                    if c >= 2:
                        pe.wait_ge(combine_read, image.count(CHUNKS, c - 1))
                    nc.tensor.matmul(combine_ps[c % 2][:, 0:PART], combine_w[:].rearrange("p i q -> p (i q)"),
                                     parts[:, c * BLOCKS:(c + 1) * BLOCKS, :].rearrange("p n v -> p (n v)"),
                                     start=True, stop=True).then_inc(combine_done, 1)
                if before:
                    tables(before, AT_ONCE)
                    tables(before, AT_ONCE + 1)
                for r in range(BITS):
                    pe.wait_ge(count_ready, image.count(BITS, r + 1))
                    nc.tensor.matmul(total_ps, ones_bf[:, :], count[:, :], start=True, stop=True)\
                      .then_inc(total_ready, 1)
                    if after and r > 8:
                        turn(after, r - 9)
                    if before and r == 16:
                        tables(before, AT_ONCE + 2)
                if after:
                    turn(after, BITS - 9)
                pe.wait_ge(ties_ready, image.count(1, 1))
                nc.tensor.matmul(above_ps, ones_bf[:, :], count[:, :], start=True, stop=True)
                flat = "q a b -> q (a b)"
                nc.tensor.matmul(before_ps, row_before[:].rearrange(flat), eq_rows[:, :], start=True, stop=False)
                nc.tensor.matmul(before_ps, band_same[:].rearrange(flat), eq_before[:, :], start=False, stop=False)
                nc.tensor.matmul(before_ps, band_before[:].rearrange(flat),
                                 eq_cum[:, CHUNKS - 1:CHUNKS].to_broadcast([P, CHUNKS]), start=False, stop=True)\
                  .then_inc(ties_added, 1)
                pe.wait_ge(gate_ready, image.count(1, 1))
                for h in (0, 1):
                    mm = nc.tensor.transpose(gate_ps[:, h * P:(h + 1) * P],
                                             gate_pad[:, 4 * h:4 * h + 4, :].rearrange("p k n -> p (k n)"), identity[:, :])
                mm.then_inc(gate_turned, 1)
                pe.wait_ge(gate_copied, image.count(1, 1))
                for n in range(AT_ONCE):
                    tables(image, n)
                if after:
                    for k in range(IMG_TURNS - LATE_TURNS, IMG_TURNS):
                        turn(after, k)

            run(phase, turn, pe)
            for n in range(AT_ONCE, CHUNKS):
                tables(Image(IMAGES // 2 - 1, 1), n)

        @block.vector
        def _(dve):
            dve.wait_ge(w_loaded, 2 * QUADS * 16)
            dve.wait_ge(const_step, CONSTS)
            for kh in (0, 1):
                for kw in (0, 1):
                    for h in (0, 1):
                        w = group_w[:, kh, kw, h]
                        ins = nc.vector.tensor_scalar(w, w, w_col[:, kh, kw, h:h + 1], None, ALU.mult)
            ins.then_inc(w_ready, 1)
            dve.wait_ge(w_summed, 1)
            nc.vector.tensor_copy(w_group[:, :], misc_ps[:, 0:GROUPS])

            def turn(image, k):
                chunk, row, h = k // TURNS, k // 2, k % 2
                if k % TURNS == 0:
                    dve.wait_ge(loaded[image.odd][chunk], image.uses(DMA_COUNT))
                if k >= 2 or not image.first:
                    dve.wait_ge(turn_done, image.count(IMG_TURNS, k - 1))
                    dve.wait_ge(part_done, image.count(IMG_TURNS, k - 1))
                src = x_row(image.odd, row).rearrange("p (m h u) -> p h m u", h=2, u=SQ)[:, h]
                dst = turned[:, k % 2, :].rearrange("p (m v) -> p m v", v=SQ)
                nc.vector.transpose(dst, src).then_inc(turn_ready, 1)

            def bulk(image, n):
                chunk = VECTOR_ORDER[n]
                views = []
                for row in (0, 1):
                    r = x_row(image.odd, 2 * chunk + row).rearrange("p (n w g t) -> p w n g t", n=BLOCKS, w=2, t=2)
                    views += [r[:, 0], r[:, 1]]

                def table(ps):
                    return ps[:, 0:PART].rearrange("p (n g) -> p n g", g=GROUPS).unsqueeze(3)\
                        .to_broadcast([P, BLOCKS, GROUPS, 2])

                k = TABLE_ORDER.index(chunk)
                for j, v in enumerate(views):
                    if j == 0:
                        dve.wait_ge(scale_ready, image.count(CHUNKS, k + 1))
                    nc.vector.tensor_tensor(v, v, table(scale_ps), ALU.mult).then_inc(vec_scaled, 1)
                    yield
                for j, v in enumerate(views):
                    if j == 0:
                        dve.wait_ge(offset_ready, image.count(CHUNKS, k + 1))
                    dve.wait_ge(vec_scaled, image.count(4 * NV, 4 * n + j + 1))
                    nc.vector.tensor_tensor(v, v, table(offset_ps), ALU.add).then_inc(vec_applied, 1)
                    yield

            def phase(image, before, after):
                steps = 0

                def chain(ins):
                    nonlocal steps
                    steps += 1
                    ins.then_inc(step, 1)
                    dve.wait_ge(step, image.count(STEPS, steps))

                def rows(t):
                    return t[:, :].rearrange("p (k n) -> p k n", n=BLOCKS)

                dve.wait_ge(turn_done, image.count(IMG_TURNS, IMG_TURNS))
                chain(nc.vector.tensor_reduce(sums2[:], sums[:], AX.X, ALU.add))
                nc.vector.tensor_tensor(group_sums[:, :, :].rearrange("p s (h g) -> p s h g", h=2),
                                        in_group[:, :].unsqueeze(1).unsqueeze(1).to_broadcast([P, 2, 2, GROUPS // 2]),
                                        sums2[:].unsqueeze(3).to_broadcast([P, 2, 2, GROUPS // 2]), ALU.mult)\
                  .then_inc(sums_ready, 1)
                dve.wait_ge(sums_added, image.count(1, 1))
                chain(nc.vector.tensor_scalar(stat[:, 0:2, :], sums_ps, 1.0 / NORM, None, ALU.mult))
                chain(nc.vector.tensor_tensor(stat[:, 3, :], stat[:, 0, :], stat[:, 0, :], ALU.mult))
                chain(nc.vector.tensor_tensor(stat[:, 4, :], stat[:, 1, :], stat[:, 3, :], ALU.subtract))
                nc.vector.tensor_scalar(stat[:, 2, :], stat[:, 4, :], 0.0, EPS, ALU.max, ALU.add).then_inc(var_ready, 1)
                dve.wait_ge(dev_ready, image.count(1, 1))
                chain(nc.vector.reciprocal(stat[:, 1, :], deviation[:, :]))
                chain(nc.vector.tensor_tensor(stat[:, 3, :], stat[:, 1, :], stat[:, 1, :], ALU.mult))
                chain(nc.vector.tensor_tensor(stat[:, 4, :], stat[:, 3, :], stat[:, 2, :], ALU.mult))
                chain(nc.vector.tensor_scalar(stat[:, 4, :], stat[:, 4, :], -0.5, 1.5, ALU.mult, ALU.add))
                nc.vector.tensor_tensor(norm_ps[:, 0, :], stat[:, 1, :], stat[:, 4, :], ALU.mult)
                chain(nc.vector.tensor_tensor(stat[:, 1, :], stat[:, 1, :], stat[:, 4, :], ALU.mult))
                chain(nc.vector.scalar_tensor_tensor(stat[:, 4, :], stat[:, 1, :], 1.0, diagonal[:, :], ALU.mult,
                                                     ALU.mult, accum_out=own[:, :]))
                nc.vector.tensor_scalar(combine_w[:], quad_same[:], own[:, 0:1], None, ALU.mult)\
                  .then_inc(combine_ready, 1)
                chain(nc.vector.scalar_tensor_tensor(stat[:, 3, :], stat[:, 0, :], -1.0, stat[:, 1, :], ALU.mult, ALU.mult))
                nc.vector.tensor_copy(norm_ps[:, 1, :], stat[:, 3, :])
                chain(nc.vector.scalar_tensor_tensor(stat[:, 4, :], stat[:, 3, :], 1.0, w_group[:, :], ALU.mult,
                                                     ALU.mult, accum_out=shift[:, :]))
                for c in range(CHUNKS):
                    dve.wait_ge(combine_done, image.count(CHUNKS, c + 1))
                    nc.vector.transpose(parts[:, c * BLOCKS:(c + 1) * BLOCKS, :],
                                        combine_ps[c % 2][:, 0:PART].rearrange("p (n v) -> p n v", v=SQ))\
                      .then_inc(combine_read, 1)
                dve.wait_ge(combine_read, image.count(CHUNKS, CHUNKS))
                nc.vector.tensor_scalar(gates[:, :], parts[:, :, 0], shift[:, 0:1], None, ALU.add).then_inc(combined, 1)
                dve.wait_ge(combined, image.count(1, 1))
                chain(nc.vector.memset(candidate[:, :], 0))
                late = bulk(before, NV - 1) if before else iter(())
                for r in range(BITS):
                    nc.vector.tensor_scalar(picked[:, :], gates[:, :], candidate[:, 0:1].bitcast(F32), None, ALU.is_ge,
                                            ALU.add, accum_out=count[:, :]).then_inc(count_ready, 1)
                    if r < 8:
                        next(late, None)
                    elif after:
                        turn(after, r - 8)
                    dve.wait_ge(total_ready, image.count(BITS, r + 1))
                    chain(nc.vector.tensor_scalar(flip[:, :], total_ps, float(TOP), float(2 ** (31 - r)) if r else -1.0,
                                                  ALU.is_lt, ALU.mult))
                    next_bit = 2 ** (30 - r) if r < BITS - 1 else 0
                    chain(nc.vector.scalar_tensor_tensor(candidate[:, :], candidate[:, :], next_bit, flip[:, :],
                                                         ALU.bitwise_xor, ALU.bitwise_xor))
                kth = candidate[:, 0:1].bitcast(F32)
                nc.vector.tensor_scalar(picked[:, :], gates[:, :], kth, None, ALU.is_gt, ALU.add, accum_out=count[:, :])
                chain(nc.vector.tensor_scalar(equal[:, :], gates[:, :], kth, None, ALU.is_equal))
                with nc.allow_low_precision("counts up to BLOCKS are exact in bfloat16"):
                    chain(nc.vector.tensor_reduce(eq_rows[:, :], rows(equal), AX.X, ALU.add))
                chain(nc.vector.tensor_tensor_scan(eq_cum[:, :], eq_rows[:, :], zeros[:, 0:CHUNKS], 0.0, ALU.add, ALU.add))
                nc.vector.tensor_tensor(eq_before[:, :], eq_cum[:, :], eq_rows[:, :], ALU.subtract).then_inc(ties_ready, 1)
                nc.vector.tensor_tensor_scan(scanned[:, :], equal[:, :], zeros[:, :], 0.0, ALU.add, ALU.add)
                dve.wait_ge(ties_added, image.count(1, 1))
                chain(nc.vector.tensor_scalar(room[:, :], above_ps, -1.0, float(TOP), ALU.mult, ALU.add))
                chain(nc.vector.tensor_tensor(limit[:, :], before_ps, eq_before[:, :], ALU.subtract))
                chain(nc.vector.tensor_scalar(limit[:, :], limit[:, :], -1.0, room[:, 0:1], ALU.mult, ALU.add))
                chain(nc.vector.tensor_tensor(rows(scanned), rows(scanned),
                                              limit[:, :].unsqueeze(2).to_broadcast([P, CHUNKS, BLOCKS]), ALU.is_le))
                chain(nc.vector.tensor_tensor(equal[:, :], equal[:, :], scanned[:, :], ALU.mult))
                chain(nc.vector.tensor_tensor(picked[:, :], picked[:, :], equal[:, :], ALU.add))
                if before:
                    dve.wait_ge(offset_ready, image.count(CHUNKS, 0))
                d = diagonal[:, 0:BLOCKS].unsqueeze(2).to_broadcast([P, BLOCKS, GROUPS])
                for j in (0, 1):
                    ins = nc.vector.tensor_tensor(spread[:, j, :, :], d, norm_ps[:, j:j + 1, :].to_broadcast([P, BLOCKS, GROUPS]),
                                                  ALU.mult)
                chain(ins)
                chain(nc.vector.tensor_scalar(spread[:, 0, :, :], spread[:, 0, :, :], diagonal[:, BLOCKS:BLOCKS + 1], None, ALU.add))
                nc.vector.tensor_tensor(gate_pad[:, 0:CHUNKS, 0:BLOCKS], rows(gates), rows(picked), ALU.mult)\
                  .then_inc(gate_ready, 1)
                dve.wait_ge(gate_turned, image.count(1, 1))
                nc.vector.tensor_copy(gate_t[:, :], gate_ps).then_inc(gate_copied, 1)
                for n in range(NV - 1):
                    for _ in bulk(image, n):
                        pass
                if after:
                    for k in range(IMG_TURNS - LATE_TURNS, IMG_TURNS):
                        turn(after, k)
                assert steps == STEPS, steps

            STEPS = 24 + 2 * BITS
            run(phase, turn, dve)
            for _ in bulk(Image(IMAGES // 2 - 1, 1), NV - 1):
                pass


def kernel(**inputs):
    import concourse.bacc as bacc
    from concourse.bass_utils import run_bass_kernel_spmd

    nc = bacc.Bacc("TRN2", target_bir_lowering=False, num_devices=1,
                    dynamic_dma_scratch_size=1024)
    arrays, args = {}, []
    for name in ("x", "L0_conv_gating_kernel"):
        a = np.ascontiguousarray(inputs[name])
        arrays[name] = a
        args.append(nc.dram_tensor(name, a.shape, mybir.dt.from_np(a.dtype), kind="ExternalInput").ap())
    args.append(nc.dram_tensor("out", arrays["x"].shape, F32, kind="ExternalOutput").ap())
    gating_kernel(nc, *args)
    return run_bass_kernel_spmd(nc, [arrays], core_ids=[0]).results[0]["out"]
```

```python
from contextlib import ExitStack

import numpy as np

import concourse.bass as bass
import concourse.mybir as mybir

F32 = mybir.dt.float32
BF16 = mybir.dt.bfloat16
I32 = mybir.dt.int32
ALU = mybir.AluOpType
ACT = mybir.ActivationFunctionType
AX = mybir.AxisListType

TOP = 1254
GROUPS = 32
EPS = 1e-5
BITS = 32


class Image:

    def __init__(self, half, odd, first=False, last=False):
        self.half, self.odd, self.first, self.last = half, odd, first, last

    def count(self, each, plus):
        return self.half * (2 * each) + (each * self.odd + plus)

    def uses(self, each):
        return self.half * each + each

    @property
    def number(self):
        return self.half * 2 + self.odd

    def next(self):
        return Image(self.half + 1, 0) if self.odd else Image(self.half, 1)


def gating_kernel(nc, x, weights, out):
    IMAGES, HEIGHT, WIDTH, CH = x.shape
    P = 128
    PA, PB = 16, 8
    ROWS = HEIGHT // PA
    CHUNKS = ROWS // 2
    BLOCKS = WIDTH // PB // 2
    STRIP = 2 * CH
    ROW = BLOCKS * STRIP
    GATES = CHUNKS * BLOCKS
    SQ = 32
    QUADS = P // SQ
    TURN = ROW // 2
    TURNS = 4
    IMG_TURNS = CHUNKS * TURNS
    PART = BLOCKS * GROUPS
    NORM = HEIGHT * WIDTH * (CH // GROUPS)
    SHARED = 2
    PRIVATE = ROWS - SHARED
    PAD = 32
    assert P == PA * PB and IMAGES % 2 == 0 and PART <= 512

    VECTOR_ORDER = [6, 2]
    POOL_CHUNKS = [0, 1, 3, 4, 5]
    LAST_VECTOR, LAST_POOL = [6, 2, 4, 5], [0, 1, 3]
    LAST_STORES = [0, 2, 4, 1, 5, 3]
    TABLE_ORDER = [6, 0, 1, 2, 3, 4, 5]
    AT_ONCE = 3
    LATE_TURNS = 7
    EARLY_TURNS = 2
    IN_ROUNDS = IMG_TURNS - LATE_TURNS - EARLY_TURNS
    ROUND_TURN = [None] * BITS
    for n in range(IN_ROUNDS - 1):
        ROUND_TURN[n * (BITS - 1) // (IN_ROUNDS - 1)] = EARLY_TURNS + n
    ROUND_TURN[-1] = IMG_TURNS - LATE_TURNS - 1
    LATE_TABLES = {4: 5, 10: 6}
    ROUND_TABLES, ROUND_PRODUCTS = [], []
    waiting = [("turn", 1, 0), ("turn", 1, 1)]
    for r in range(BITS):
        if r in LATE_TABLES:
            waiting = [("table", LATE_TABLES[r], 0), ("table", LATE_TABLES[r], 1)] + waiting
        at_once = 2 if ROUND_TURN[r] is not None else 1
        ROUND_TABLES.append([w[1:] for w in waiting[:at_once] if w[0] == "table"])
        ROUND_PRODUCTS.append([w[1:] for w in waiting[:at_once] if w[0] == "turn"])
        waiting = waiting[at_once:]
        if ROUND_TURN[r] is not None:
            waiting += [("turn", ROUND_TURN[r], 0), ("turn", ROUND_TURN[r], 1)]
    LAST_PRODUCTS = [w[1:] for w in waiting]

    AFTER_GATES = [21] + ["apply"] * 8 + [22] + ["apply"] * 8 + [23, 24, 25, 26, 27]
    ACT_TABLES_LATE = {0: 2, 5: 3, 10: 4}

    ctx = ExitStack()
    with ctx:
        def sb(name, shape, dt=F32):
            return ctx.enter_context(nc.sbuf_tensor(name, shape, dt))

        def psum(name, shape, dt=F32):
            return ctx.enter_context(nc.psum_tensor(name, shape, dt))

        def sem(name):
            return ctx.enter_context(nc.semaphore(name))

        def parts_of(row):
            return (0, 1) if row >= PRIVATE else (0,)

        def blocks_of(row, part):
            each = BLOCKS // len(parts_of(row))
            return slice(part * each, (part + 1) * each)

        xbuf = sb("xbuf", [P, 2 * PRIVATE + SHARED, ROW])
        parts = sb("parts", [P, GATES, GROUPS])
        turned = sb("turned", [P, 2, TURN])
        unused = sb("unused", [P, 2, TURN], BF16)
        pool_tables = sb("pool_tables", [P, 2, PART])
        spread = sb("spread", [P, 2, BLOCKS, GROUPS])
        identity = sb("identity", [P, P])
        one = sb("one", [P, 1])
        ones_bf = sb("ones_bf", [P, P], BF16)
        row_before = sb("row_before", [P, PA, PB], BF16)
        band_same = sb("band_same", [P, PA, PB], BF16)
        band_before = sb("band_before", [P, PA, PB], BF16)
        quad_same = sb("quad_same", [P, QUADS])
        combine_w = sb("combine_w", [P, CHUNKS - 1 + P])
        in_group = sb("in_group", [P, GROUPS // 2])
        group_w = sb("group_w", [P, 2, 2, 2, QUADS, GROUPS])
        diagonal = sb("diagonal", [P, SQ])
        w_col = sb("w_col", [P, 2, 2, 2])
        w_group = sb("w_group", [P, GROUPS])
        gate_pad = sb("gate_pad", [P, CHUNKS, PAD])
        gate_t = sb("gate_t", [P, 2 * P])
        sums = sb("sums", [P, 2, 2, ROWS])
        sums2 = sb("sums2", [P, 2, 2])
        own = sb("own", [P, 1])
        group_sums = sb("group_sums", [P, 2, GROUPS])
        stat = sb("stat", [P, 5, GROUPS])
        deviation = sb("deviation", [P, GROUPS])
        shift = sb("shift", [P, 1])
        gates = sb("gates", [P, GATES])
        picked = sb("picked", [P, GATES], BF16)
        equal = sb("equal", [P, GATES], BF16)
        scanned = sb("scanned", [P, GATES], BF16)
        candidate = sb("candidate", [P, 1], I32)
        flip = sb("flip", [P, 1], I32)
        count = sb("count", [P, 1], BF16)
        eq = sb("eq", [P, 3, CHUNKS], BF16)
        eq_rows, eq_cum, eq_before = eq[:, 0], eq[:, 1], eq[:, 2]
        room = sb("room", [P, 1])
        limit = sb("limit", [P, CHUNKS])

        scale_ps = [psum(f"scale_ps{i}", [P, 512]) for i in range(2)]
        offset_ps = [psum(f"offset_ps{i}", [P, 512]) for i in range(2)]
        parts_ps = [psum(f"parts_ps{i}", [P, 512]) for i in range(2)]
        misc_ps = psum("misc_ps", [P, 512])
        sums_ps = misc_ps[:, 0:2 * GROUPS].rearrange("p (s g) -> p s g", s=2)
        total_ps = misc_ps[:, 128:129]
        above_ps = misc_ps[:, 129:130]
        before_ps = misc_ps[:, 136:136 + CHUNKS]
        gate_ps = misc_ps[:, 256:512]

        w_loaded = sem("w_loaded")
        settled = sem("settled")
        loaded = [[[sem(f"loaded{o}_{r}_{p}") for p in parts_of(r)] for r in range(ROWS)] for o in range(2)]
        stored = [[[sem(f"stored{o}_{r}_{p}") for p in parts_of(r)] for r in range(ROWS)] for o in range(2)]
        const_step = sem("const_step")
        w_ready = sem("w_ready")
        w_summed = sem("w_summed")
        turn_ready = sem("turn_ready")
        turn_done = sem("turn_done")
        part_done = sem("part_done")
        combine_ready = sem("combine_ready")
        combine_done = sem("combine_done")
        combine_read = sem("combine_read")
        norm_ready = sem("norm_ready")
        spread_ready = sem("spread_ready")
        spread_step = sem("spread_step")
        parts_copied = sem("parts_copied")
        sums_ready = sem("sums_ready")
        sums_added = sem("sums_added")
        var_ready = sem("var_ready")
        dev_ready = sem("dev_ready")
        step = sem("step")
        combined = sem("combined")
        count_ready = sem("count_ready")
        total_ready = sem("total_ready")
        ties_ready = sem("ties_ready")
        ties_added = sem("ties_added")
        gate_ready = sem("gate_ready")
        gate_turned = sem("gate_turned")
        gate_copied = sem("gate_copied")
        scale_ready = sem("scale_ready")
        offset_ready = sem("offset_ready")
        vec_scaled = sem("vec_scaled")
        vec_applied = sem("vec_applied")
        tables_copied = sem("tables_copied")
        pool_scaled = sem("pool_scaled")
        pool_applied = sem("pool_applied")

        NP = len(POOL_CHUNKS)

        LAST = Image(IMAGES // 2 - 1, 1, last=True)

        def vector_chunks(image):
            return LAST_VECTOR if image.last else VECTOR_ORDER

        def pool_chunks(image):
            return LAST_POOL if image.last else POOL_CHUNKS

        def slot(odd, row):
            return ROWS + row if odd and row < PRIVATE else row

        def x_row(odd, row):
            return xbuf[:, slot(odd, row), :]

        DMA_COUNT = 16

        def in_dram(t, image, row, part):
            v = t[image.number].rearrange("(a t) (b w) c -> a b t (w c)", a=PA, b=PB)
            blocks = blocks_of(row, part)
            return v[:, :, row, blocks.start * STRIP:blocks.stop * STRIP]

        def in_sbuf(odd, row, part):
            blocks = blocks_of(row, part)
            return x_row(odd, row)[:, blocks.start * STRIP:blocks.stop * STRIP]

        def pieces(chunk):
            return [(row, part) for row in (2 * chunk, 2 * chunk + 1) for part in parts_of(row)]

        def applied_before(chunks, chunk):
            return sum(2 * len(pieces(c)) for c in chunks[:chunks.index(chunk)])

        VEC_COUNT = sum(2 * len(pieces(c)) for c in VECTOR_ORDER)
        POOL_COUNT = sum(2 * len(pieces(c)) for c in POOL_CHUNKS)

        def table_bank(image, n):
            return (n + CHUNKS * image.odd) % 2

        def combine_bank(image):
            return (CHUNKS - 1 + CHUNKS * image.odd) % 2

        def run(phase, turns, eng):
            last = IMAGES // 2 - 1
            first = Image(0, 0, True)
            if turns:
                for k in range(IMG_TURNS):
                    turns(first, k)
            phase(first, None, Image(0, 1))
            with eng.Fori(0, last) as t:
                phase(Image(t, 1), Image(t, 0), Image(t + 1, 0))
                phase(Image(t + 1, 0), Image(t, 1), Image(t + 1, 1))
            phase(LAST, Image(last, 0), None)

        block = ctx.enter_context(nc.Block())

        @block.sync
        def _(sp):
            with nc.allow_non_contiguous_dma("256 weights, once"):
                for i in range(QUADS):
                    for kh in range(2):
                        sp.dma_start(w_col[i * SQ:(i + 1) * SQ, kh], weights[kh].rearrange(
                            "kw (h u) o -> u kw (h o)", u=SQ)).then_inc(w_loaded, 16)

            def settle():
                sp.sem_inc(settled, 1)

            def load(image, row, part):
                sp.dma_start(in_sbuf(image.odd, row, part), in_dram(x, image, row, part))\
                  .then_inc(loaded[image.odd][row][part], DMA_COUNT)

            def store(image, row, part):
                chunk = row // 2
                done = 2 * pieces(chunk).index((row, part)) + 2
                if chunk in pool_chunks(image):
                    sp.wait_ge(pool_applied, image.count(POOL_COUNT, applied_before(pool_chunks(image), chunk) + done))
                else:
                    sp.wait_ge(vec_applied, image.count(VEC_COUNT, applied_before(vector_chunks(image), chunk) + done))
                settle()
                sp.dma_start(in_dram(out, image, row, part), in_sbuf(image.odd, row, part))\
                  .then_inc(stored[image.odd][row][part], DMA_COUNT)

            def freed(image, row, part):
                sp.wait_ge(stored[image.odd][row][part], image.uses(DMA_COUNT))
                settle()

            def phase(image, load1, load2):
                image1 = image.next()
                image2 = image1.next()
                shared = pieces(CHUNKS - 1)
                for n in range(len(shared) + 2):
                    if n >= 2 and load1:
                        freed(image, *shared[n - 2])
                        load(image1, *shared[n - 2])
                    if n < len(shared):
                        store(image, *shared[n])
                for c in LAST_STORES if image.last else range(CHUNKS - 1):
                    for piece in pieces(c):
                        store(image, *piece)
                    if load2:
                        for piece in pieces(c):
                            freed(image, *piece)
                            load(image2, *piece)

            first, second = Image(0, 0, True), Image(0, 1)
            for c in range(CHUNKS):
                for piece in pieces(c):
                    load(first, *piece)
            for c in range(CHUNKS - 1):
                for piece in pieces(c):
                    load(second, *piece)
            phase(first, True, True)
            last = IMAGES // 2 - 1
            with sp.Fori(0, last - 1) as t:
                phase(Image(t, 1), True, True)
                phase(Image(t + 1, 0), True, True)
            phase(Image(last - 1, 1), True, True)
            phase(Image(last, 0), True, False)
            phase(LAST, False, False)
            for odd in range(2):
                for c in range(CHUNKS):
                    for piece in pieces(c):
                        freed(Image(last, odd), *piece)

        W_CONSTS = 3 + 2 + 8
        CONSTS = W_CONSTS + 9 + 1 + 4 + 5 + 1

        @block.gpsimd
        def _(pool):
            n = 0

            def done(ins):
                nonlocal n
                n += 1
                ins.then_inc(const_step, 1)
                pool.wait_ge(const_step, n)

            def keep(t, base, step_q, pattern):
                done(nc.gpsimd.affine_select(out=t, in_=t, compare_op=ALU.is_ge, fill=0.0, base=base,
                                             pattern=pattern, channel_multiplier=step_q))

            def one_at_zero(t, base, pattern):
                done(nc.gpsimd.affine_select(out=t, in_=t, compare_op=ALU.not_equal, fill=1.0, base=base,
                                             pattern=pattern, channel_multiplier=1))

            for t, v in ((group_w, 0.0), (quad_same, 1.0), (in_group, 1.0)):
                done(nc.gpsimd.memset(t[:], v))
            keep(quad_same[:, :], 0, 1, [[-SQ, QUADS]])
            keep(quad_same[:, :], SQ - 1, -1, [[SQ, QUADS]])
            for j in range(0, P, 32):
                keep(in_group[j:j + 32, :], 0, 1, [[-2, GROUPS // 2]])
                keep(in_group[j:j + 32, :], 1, -1, [[2, GROUPS // 2]])
            assert n == W_CONSTS, n
            for t, v in ((identity, 0.0), (one, 1.0), (ones_bf, 1.0), (row_before, 1.0), (band_same, 1.0),
                         (band_before, 1.0), (diagonal, 0.0), (gate_pad, 0.0), (combine_w, 0.0)):
                done(nc.gpsimd.memset(t[:], v))
            one_at_zero(identity[:, :], 0, [[-1, P]])
            for j in range(0, P, 32):
                one_at_zero(diagonal[j:j + 32, :], 0, [[-1, SQ]])
            keep(band_same[:], 0, 1, [[-PB, PA], [0, PB]])
            keep(band_same[:], PB - 1, -1, [[PB, PA], [0, PB]])
            keep(row_before[:], 0, 1, [[-PB, PA], [0, PB]])
            keep(row_before[:], -1, -1, [[PB, PA], [1, PB]])
            keep(band_before[:], -1, -1, [[PB, PA], [0, PB]])
            done(nc.gpsimd.memset(gate_pad[:, :, BLOCKS:BLOCKS + 1], 1.0))

            def view(odd, row, w):
                return x_row(odd, row).rearrange("p (n w g t) -> p w n g t", n=BLOCKS, w=2, t=2)[:, w]

            def table(j):
                return pool_tables[:, j, :].rearrange("p (n g) -> p n g", g=GROUPS).unsqueeze(3)\
                    .to_broadcast([P, BLOCKS, GROUPS, 2])

            def phase(image):
                pool.wait_ge(norm_ready, image.count(1, 1))
                if not image.first:
                    pool.wait_ge(offset_ready, image.count(CHUNKS, 0))
                d = diagonal[:, 0:BLOCKS].unsqueeze(2).to_broadcast([P, BLOCKS, GROUPS])
                for j, row in ((0, 1), (1, 3)):
                    factor = stat[:, row:row + 1, :].to_broadcast([P, BLOCKS, GROUPS])
                    ins = nc.gpsimd.tensor_tensor(spread[:, j, :, :], d, factor, ALU.mult)
                ins.then_inc(spread_step, 1)
                pool.wait_ge(spread_step, image.count(1, 1))
                nc.gpsimd.tensor_tensor(spread[:, 0, :, :], spread[:, 0, :, :],
                                        diagonal[:, BLOCKS:BLOCKS + 1].unsqueeze(2).to_broadcast([P, BLOCKS, GROUPS]),
                                        ALU.add).then_inc(spread_ready, 1)
                for k, chunk in enumerate(pool_chunks(image)):
                    for second in (0, 1):
                        row = 2 * chunk + second
                        if not second:
                            pool.wait_ge(tables_copied, image.count(2 * NP, 2 * k + 1))
                        for w in (0, 1):
                            v = view(image.odd, row, w)
                            nc.gpsimd.tensor_tensor(v, v, table(0), ALU.mult).then_inc(pool_scaled, 1)
                        if not second:
                            pool.wait_ge(tables_copied, image.count(2 * NP, 2 * k + 2))
                        for w in (0, 1):
                            v = view(image.odd, row, w)
                            pool.wait_ge(pool_scaled, image.count(4 * NP, 4 * k + 2 * second + w + 1))
                            nc.gpsimd.tensor_tensor(v, v, table(1), ALU.add).then_inc(pool_applied, 1)

            assert n == CONSTS, n
            last = IMAGES // 2 - 1
            with pool.Fori(0, last) as t:
                phase(Image(t, 0))
                phase(Image(t, 1))
            phase(Image(last, 0))
            phase(LAST)

        @block.scalar
        def _(act):
            def turn(image, k):
                y, row, h = turned[:, k % 2, :], k // 2, k % 2
                act.wait_ge(turn_ready, image.count(IMG_TURNS, k + 1))
                if k or not image.first:
                    act.wait_ge(turn_done, image.count(IMG_TURNS, k))
                nc.scalar.activation(unused[:, 0, :], y, ACT.Identity, accum_out=sums[:, 0, h, row:row + 1])
                nc.scalar.activation(unused[:, 1, :], y, ACT.Square,
                                     accum_out=sums[:, 1, h, row:row + 1]).then_inc(turn_done, 1)
                if k % TURNS == 1 and k > 1:
                    copy_parts(image, k // TURNS - 1)
                if k == IMG_TURNS - 1:
                    copy_parts(image, CHUNKS - 1)

            def copy_parts(image, c):
                act.wait_ge(part_done, image.count(IMG_TURNS, TURNS * (c + 1)))
                if c == 0 and not image.first:
                    act.wait_ge(combined, image.count(1, 0))
                nc.scalar.activation(parts[:, c * BLOCKS:(c + 1) * BLOCKS, :],
                                     parts_ps[(c + image.odd * CHUNKS) % 2][:, 0:PART]
                                     .rearrange("p (n g) -> p n g", g=GROUPS),
                                     ACT.Identity).then_inc(parts_copied, 1)

            def pool_tables_copy(image, k):
                n = TABLE_ORDER.index(POOL_CHUNKS[k])
                for ready, ps, j, through in ((scale_ready, scale_ps, 0, pool_scaled),
                                              (offset_ready, offset_ps, 1, pool_applied)):
                    if k or not image.first:
                        act.wait_ge(through, image.count(4 * NP, 4 * k))
                    act.wait_ge(ready, image.count(CHUNKS, n + 1))
                    nc.scalar.activation(pool_tables[:, j, :], ps[table_bank(image, n)][:, 0:PART], ACT.Identity)\
                      .then_inc(tables_copied, 1)

            def phase(image, before, after):
                act.wait_ge(var_ready, image.count(1, 1))
                nc.scalar.activation(deviation[:, :], stat[:, 2, :], ACT.Sqrt).then_inc(dev_ready, 1)
                for k in range(IMG_TURNS - LATE_TURNS):
                    if before and k in ACT_TABLES_LATE:
                        pool_tables_copy(before, ACT_TABLES_LATE[k])
                    if after:
                        turn(after, k)
                for k in range(IMG_TURNS - LATE_TURNS, IMG_TURNS):
                    if k == IMG_TURNS - LATE_TURNS + 1:
                        pool_tables_copy(image, 0)
                    if k == IMG_TURNS - 2:
                        pool_tables_copy(image, 1)
                    if after:
                        turn(after, k)

            run(phase, turn, act)
            for k in range(2, len(LAST_POOL)):
                pool_tables_copy(LAST, k)

        @block.tensor
        def _(pe):
            pe.wait_ge(const_step, CONSTS)
            pe.wait_ge(w_ready, 1)
            ones = one[:, 0:1].to_broadcast([P, P])
            for n in range(8):
                w = group_w[:, n // 4, n // 2 % 2, n % 2].rearrange("p i g -> p (i g)")
                mm = nc.tensor.matmul(misc_ps[:, 0:P], ones, w, start=n == 0, stop=n == 7)
            mm.then_inc(w_summed, 1)

            def turn(image, k, halves=(0, 1)):
                chunk, row, h = k // TURNS, k // 2 % 2, k % 2
                if k % TURNS == 0 and (chunk >= 2 or not image.first):
                    pe.wait_ge(parts_copied, image.count(CHUNKS, chunk - 1))
                pe.wait_ge(turn_ready, image.count(IMG_TURNS, k + 1))
                y = turned[:, k % 2, :].rearrange("p (n w v) -> p w n v", w=2, v=SQ)
                for kw in halves:
                    mm = nc.tensor.matmul(parts_ps[(chunk + image.odd * CHUNKS) % 2][:, 0:PART],
                                          group_w[:, row, kw, h].rearrange("p i g -> p (i g)"), y[:, kw],
                                          start=(k % TURNS == 0 and kw == 0), stop=(k % TURNS == TURNS - 1 and kw == 1))
                if 1 in halves:
                    mm.then_inc(part_done, 1)

            def tables(image, n, which=(0, 1)):
                chunk = TABLE_ORDER[n]
                half = chunk // 4
                q = chunk - 3 * half
                for j in which:
                    ready, ps = ((scale_ready, scale_ps), (offset_ready, offset_ps))[j]
                    if n >= 2 or not image.first:
                        prev, ago = TABLE_ORDER[n - 2], 0 if n >= 2 else 1
                        if prev in POOL_CHUNKS:
                            pe.wait_ge(tables_copied, image.count(2 * NP, 2 * POOL_CHUNKS.index(prev) + j + 1 - 2 * NP * ago))
                        else:
                            done = applied_before(VECTOR_ORDER, prev) + 2 * len(pieces(prev))
                            pe.wait_ge(vec_scaled if j == 0 else vec_applied,
                                       image.count(VEC_COUNT, done - VEC_COUNT * ago))
                    nc.tensor.matmul(ps[table_bank(image, n)][:, 0:PART],
                                     gate_t[q * 32:q * 32 + BLOCKS + 1, half * P:(half + 1) * P],
                                     spread[q * 32:q * 32 + BLOCKS + 1, j, :, :].rearrange("p n g -> p (n g)"),
                                     start=True, stop=True).then_inc(ready, 1)

            def phase(image, before, after):
                pe.wait_ge(sums_ready, image.count(1, 1))
                nc.tensor.matmul(misc_ps[:, 0:2 * GROUPS], ones, group_sums[:, :, :].rearrange("p s g -> p (s g)"),
                                 start=True, stop=True).then_inc(sums_added, 1)
                if before:
                    tables(before, AT_ONCE)
                    tables(before, AT_ONCE + 1)
                if after:
                    turn(after, 0)
                pe.wait_ge(combine_ready, image.count(1, 1))
                pe.wait_ge(parts_copied, image.count(CHUNKS, CHUNKS))
                for c in range(CHUNKS):
                    mm = nc.tensor.matmul(parts_ps[combine_bank(image)][:, 0:PART],
                                          combine_w[:, CHUNKS - 1 - c:CHUNKS - 1 - c + P],
                                          parts[:, c * BLOCKS:(c + 1) * BLOCKS, :].rearrange("p n v -> p (n v)"),
                                          start=c == 0, stop=c == CHUNKS - 1)
                mm.then_inc(combine_done, 1)
                for r in range(BITS):
                    pe.wait_ge(count_ready, image.count(BITS, r + 1))
                    nc.tensor.matmul(total_ps, ones_bf[:, :], count[:, :], start=True, stop=True)\
                      .then_inc(total_ready, 1)
                    if before:
                        for n, j in ROUND_TABLES[r]:
                            tables(before, n, (j,))
                    if after:
                        for k, kw in ROUND_PRODUCTS[r]:
                            turn(after, k, (kw,))
                pe.wait_ge(ties_ready, image.count(1, 1))
                nc.tensor.matmul(above_ps, ones_bf[:, :], count[:, :], start=True, stop=True)
                flat = "q a b -> q (a b)"
                nc.tensor.matmul(before_ps, row_before[:].rearrange(flat), eq_rows[:, :], start=True, stop=False)
                nc.tensor.matmul(before_ps, band_same[:].rearrange(flat), eq_before[:, :], start=False, stop=False)
                nc.tensor.matmul(before_ps, band_before[:].rearrange(flat),
                                 eq_cum[:, CHUNKS - 1:CHUNKS].to_broadcast([P, CHUNKS]), start=False, stop=True)\
                  .then_inc(ties_added, 1)
                if after:
                    for k, kw in LAST_PRODUCTS:
                        turn(after, k, (kw,))
                pe.wait_ge(gate_ready, image.count(1, 1))
                for h in (0, 1):
                    mm = nc.tensor.transpose(gate_ps[:, h * P:(h + 1) * P],
                                             gate_pad[:, 3 * h:3 * h + 4, :].rearrange("p k n -> p (k n)"), identity[:, :])
                mm.then_inc(gate_turned, 1)
                pe.wait_ge(gate_copied, image.count(1, 1))
                pe.wait_ge(spread_ready, image.count(1, 1))
                tables(image, 0)
                tables(image, 1)
                for k in range(IMG_TURNS - LATE_TURNS, IMG_TURNS):
                    if k == IMG_TURNS - LATE_TURNS + 2:
                        tables(image, 2)
                    if after:
                        turn(after, k)

            run(phase, turn, pe)
            for n in range(AT_ONCE, CHUNKS):
                tables(LAST, n)

        @block.vector
        def _(dve):
            dve.wait_ge(w_loaded, 2 * QUADS * 16)
            dve.wait_ge(const_step, W_CONSTS)
            half = [P, QUADS, GROUPS // 2]
            for kh in (0, 1):
                for kw in (0, 1):
                    for h in (0, 1):
                        ins = nc.vector.scalar_tensor_tensor(
                            group_w[:, kh, kw, h, :, h * GROUPS // 2:(h + 1) * GROUPS // 2],
                            quad_same[:, :].unsqueeze(2).to_broadcast(half), w_col[:, kh, kw, h:h + 1],
                            in_group[:, :].unsqueeze(1).to_broadcast(half), ALU.mult, ALU.mult)
            ins.then_inc(w_ready, 1)
            dve.wait_ge(w_summed, 1)
            nc.vector.tensor_copy(w_group[:, :], misc_ps[:, 0:GROUPS])
            dve.wait_ge(const_step, CONSTS)

            def turn(image, k):
                row, h = k // 2, k % 2
                if h == 0:
                    for part in parts_of(row):
                        dve.wait_ge(loaded[image.odd][row][part], image.uses(DMA_COUNT))
                if k >= 2 or not image.first:
                    dve.wait_ge(turn_done, image.count(IMG_TURNS, k - 1))
                    dve.wait_ge(part_done, image.count(IMG_TURNS, k - 1))
                src = x_row(image.odd, row).rearrange("p (m h u) -> p h m u", h=2, u=SQ)[:, h]
                dst = turned[:, k % 2, :].rearrange("p (m v) -> p m v", v=SQ)
                nc.vector.transpose(dst, src).then_inc(turn_ready, 1)

            def bulk(image, n):
                chunk = vector_chunks(image)[n]
                k = TABLE_ORDER.index(chunk)
                count = applied_before(vector_chunks(image), chunk)

                def view(row, w, blocks):
                    return x_row(image.odd, row).rearrange("p (n w g t) -> p w n g t", n=BLOCKS, w=2, t=2)[:, w, blocks]

                def table(ps, blocks):
                    t = ps[table_bank(image, k)][:, 0:PART].rearrange("p (n g) -> p n g", g=GROUPS)[:, blocks]
                    return t.unsqueeze(3).to_broadcast([P, blocks.stop - blocks.start, GROUPS, 2])

                for m, (row, part) in enumerate(pieces(chunk)):
                    blocks = blocks_of(row, part)
                    if m == 0:
                        dve.wait_ge(scale_ready, image.count(CHUNKS, k + 1))
                    for w in (0, 1):
                        v = view(row, w, blocks)
                        nc.vector.tensor_tensor(v, v, table(scale_ps, blocks), ALU.mult).then_inc(vec_scaled, 1)
                        yield
                    if m == 0:
                        dve.wait_ge(offset_ready, image.count(CHUNKS, k + 1))
                    for w in (0, 1):
                        v = view(row, w, blocks)
                        dve.wait_ge(vec_scaled, image.count(VEC_COUNT, count + 2 * m + w + 1))
                        nc.vector.tensor_tensor(v, v, table(offset_ps, blocks), ALU.add).then_inc(vec_applied, 1)
                        yield

            def phase(image, before, after):
                steps = 0

                def chain(ins):
                    nonlocal steps
                    steps += 1
                    ins.then_inc(step, 1)
                    dve.wait_ge(step, image.count(STEPS, steps))

                def rows(t):
                    return t[:, :].rearrange("p (k n) -> p k n", n=BLOCKS)

                late = bulk(before, len(VECTOR_ORDER) - 1) if before else iter(())
                dve.wait_ge(turn_done, image.count(IMG_TURNS, IMG_TURNS))
                chain(nc.vector.tensor_reduce(sums2[:], sums[:], AX.X, ALU.add))
                nc.vector.tensor_tensor(group_sums[:, :, :].rearrange("p s (h g) -> p s h g", h=2),
                                        in_group[:, :].unsqueeze(1).unsqueeze(1).to_broadcast([P, 2, 2, GROUPS // 2]),
                                        sums2[:].unsqueeze(3).to_broadcast([P, 2, 2, GROUPS // 2]), ALU.mult)\
                  .then_inc(sums_ready, 1)
                dve.wait_ge(sums_added, image.count(1, 1))
                chain(nc.vector.tensor_scalar(stat[:, 0:2, :], sums_ps, 1.0 / NORM, None, ALU.mult))
                chain(nc.vector.tensor_tensor(stat[:, 3, :], stat[:, 0, :], stat[:, 0, :], ALU.mult))
                chain(nc.vector.tensor_tensor(stat[:, 4, :], stat[:, 1, :], stat[:, 3, :], ALU.subtract))
                nc.vector.tensor_scalar(stat[:, 2, :], stat[:, 4, :], 0.0, EPS, ALU.max, ALU.add).then_inc(var_ready, 1)
                if after:
                    turn(after, 0)
                dve.wait_ge(dev_ready, image.count(1, 1))
                chain(nc.vector.reciprocal(stat[:, 1, :], deviation[:, :]))
                chain(nc.vector.tensor_tensor(stat[:, 3, :], stat[:, 1, :], stat[:, 1, :], ALU.mult))
                chain(nc.vector.tensor_tensor(stat[:, 4, :], stat[:, 3, :], stat[:, 2, :], ALU.mult))
                chain(nc.vector.tensor_scalar(stat[:, 4, :], stat[:, 4, :], -0.5, 1.5, ALU.mult, ALU.add))
                chain(nc.vector.tensor_tensor(stat[:, 1, :], stat[:, 1, :], stat[:, 4, :], ALU.mult))
                chain(nc.vector.scalar_tensor_tensor(stat[:, 4, :], stat[:, 1, :], 1.0, diagonal[:, :], ALU.mult,
                                                     ALU.mult, accum_out=own[:, :]))
                nc.vector.tensor_scalar(combine_w[:, CHUNKS - 1:CHUNKS - 1 + P:SQ], quad_same[:, :], own[:, 0:1], None, ALU.mult)\
                  .then_inc(combine_ready, 1)
                nc.vector.scalar_tensor_tensor(stat[:, 3, :], stat[:, 0, :], -1.0, stat[:, 1, :], ALU.mult, ALU.mult)\
                  .then_inc(norm_ready, 1)
                dve.wait_ge(norm_ready, image.count(1, 1))
                chain(nc.vector.scalar_tensor_tensor(stat[:, 4, :], stat[:, 3, :], 1.0, w_group[:, :], ALU.mult,
                                                     ALU.mult, accum_out=shift[:, :]))
                for _ in range(2):
                    next(late, None)
                if after:
                    turn(after, 1)
                for _ in range(4):
                    next(late, None)
                dve.wait_ge(combine_done, image.count(1, 1))
                nc.vector.transpose(parts[:, 0:BLOCKS, :], parts_ps[combine_bank(image)][:, 0:PART].rearrange("p (n v) -> p n v", v=SQ))\
                  .then_inc(combine_read, 1)
                dve.wait_ge(combine_read, image.count(1, 1))
                nc.vector.tensor_scalar(rows(gates), parts[:, 0:BLOCKS, 0:CHUNKS].rearrange("p n k -> p k n"),
                                        shift[:, 0:1], None, ALU.add).then_inc(combined, 1)
                dve.wait_ge(combined, image.count(1, 1))
                chain(nc.vector.memset(candidate[:, :], 0))
                for r in range(BITS):
                    nc.vector.tensor_scalar(picked[:, :], gates[:, :], candidate[:, 0:1].bitcast(F32), None, ALU.is_ge,
                                            ALU.add, accum_out=count[:, :]).then_inc(count_ready, 1)
                    if ROUND_TURN[r] is None:
                        next(late, None)
                    elif after:
                        turn(after, ROUND_TURN[r])
                    dve.wait_ge(total_ready, image.count(BITS, r + 1))
                    chain(nc.vector.tensor_scalar(flip[:, :], total_ps, float(TOP), float(2 ** (31 - r)) if r else -1.0,
                                                  ALU.is_lt, ALU.mult))
                    next_bit = 2 ** (30 - r) if r < BITS - 1 else 0
                    chain(nc.vector.scalar_tensor_tensor(candidate[:, :], candidate[:, :], next_bit, flip[:, :],
                                                         ALU.bitwise_xor, ALU.bitwise_xor))
                kth = candidate[:, 0:1].bitcast(F32)
                nc.vector.tensor_scalar(picked[:, :], gates[:, :], kth, None, ALU.is_gt, ALU.add, accum_out=count[:, :])
                chain(nc.vector.tensor_scalar(equal[:, :], gates[:, :], kth, None, ALU.is_equal))
                with nc.allow_low_precision("counts up to BLOCKS are exact in bfloat16"):
                    chain(nc.vector.tensor_reduce(eq_rows[:, :], rows(equal), AX.X, ALU.add))
                chain(nc.vector.tensor_tensor_scan(eq_cum[:, :], eq_rows[:, :], eq_rows[:, :], 0.0, ALU.add, ALU.max))
                nc.vector.tensor_tensor(eq_before[:, :], eq_cum[:, :], eq_rows[:, :], ALU.subtract).then_inc(ties_ready, 1)
                nc.vector.tensor_tensor_scan(scanned[:, :], equal[:, :], equal[:, :], 0.0, ALU.add, ALU.max)
                dve.wait_ge(ties_added, image.count(1, 1))
                chain(nc.vector.tensor_scalar(room[:, :], above_ps, -1.0, float(TOP), ALU.mult, ALU.add))
                chain(nc.vector.tensor_tensor(limit[:, :], before_ps, eq_before[:, :], ALU.subtract))
                chain(nc.vector.tensor_scalar(limit[:, :], limit[:, :], -1.0, room[:, 0:1], ALU.mult, ALU.add))
                chain(nc.vector.tensor_tensor(rows(scanned), rows(scanned),
                                              limit[:, :].unsqueeze(2).to_broadcast([P, CHUNKS, BLOCKS]), ALU.is_le))
                chain(nc.vector.tensor_tensor(equal[:, :], equal[:, :], scanned[:, :], ALU.mult))
                chain(nc.vector.tensor_tensor(picked[:, :], picked[:, :], equal[:, :], ALU.add))
                nc.vector.tensor_tensor(gate_pad[:, 0:CHUNKS, 0:BLOCKS], rows(gates), rows(picked), ALU.mult)\
                  .then_inc(gate_ready, 1)
                dve.wait_ge(gate_turned, image.count(1, 1))
                nc.vector.tensor_copy(gate_t[:, :], gate_ps).then_inc(gate_copied, 1)
                first = bulk(image, 0)
                for what in AFTER_GATES:
                    if what == "apply":
                        next(first)
                    elif after:
                        turn(after, what)
                assert steps == STEPS, steps

            STEPS = 21 + 2 * BITS
            run(phase, turn, dve)
            for n in range(1, len(LAST_VECTOR)):
                for _ in bulk(LAST, n):
                    pass


def kernel(**inputs):
    import concourse.bacc as bacc
    from concourse.bass_utils import run_bass_kernel_spmd

    nc = bacc.Bacc("TRN2", target_bir_lowering=False, num_devices=1,
                    dynamic_dma_scratch_size=1024)
    arrays, args = {}, []
    for name in ("x", "L0_conv_gating_kernel"):
        a = np.ascontiguousarray(inputs[name])
        arrays[name] = a
        args.append(nc.dram_tensor(name, a.shape, mybir.dt.from_np(a.dtype), kind="ExternalInput").ap())
    args.append(nc.dram_tensor("out", arrays["x"].shape, F32, kind="ExternalOutput").ap())
    gating_kernel(nc, *args)
    return run_bass_kernel_spmd(nc, [arrays], core_ids=[0]).results[0]["out"]
```
